# Optimizing a Trainium2 kernel written in Bass

```python
import numpy as np
import jax
import jax.numpy as jnp

def _softmax(x, axis=-1):
    return jax.nn.softmax(x, axis=axis)

def _gelu(x):
    return jax.nn.gelu(x, approximate=True)

def _silu(x):
    return jax.nn.silu(x)

def _sigmoid(x):
    return jax.nn.sigmoid(x)

def _layernorm(x, axis=-1, eps=1e-05):
    m = jnp.mean(x, axis=axis, keepdims=True)
    v = jnp.var(x, axis=axis, keepdims=True)
    return (x - m) / jnp.sqrt(v + eps)

def _scatter_add(tgt, idx, src, axis=0):
    return tgt.at[idx].add(src)

def _segment_sum(src, seg, n):
    return jax.ops.segment_sum(src, seg, n)
kernel_name = 'mk_adj_resnorm_d2_adj_r2_72a3b2'

def setup_inputs(seed: int=0):
    np.random.seed(seed)
    _w = jnp.asarray

    def _rec_inputs():
        import jax
        import jax.numpy as jnp
        _gk = jax.random.key(seed)
        x = -0.0005207 + 1.001 * jax.random.normal(jax.random.fold_in(_gk, 1), (4096, 128), jnp.float32)
        _a = jax.random.bernoulli(jax.random.fold_in(_gk, 2), 0.000976562, (4096, 4096))
        _a = jnp.logical_or(_a, jnp.swapaxes(_a, -1, -2))
        _a = jnp.logical_or(_a, jnp.eye(4096, dtype=bool))
        _af = _a.astype(jnp.float32)
        adj = _af
        return (x, adj)
    x, adj = _rec_inputs()

    def _L0_gnn_setup():
        import jax, jax.numpy as jnp
        import numpy as np
        NEG_BIG = -9000000000000000.0
        ALPHA = 0.2
        key = jax.random.key(seed)
        k1, k2, k3, k4 = jax.random.split(key, 4)
        N, F_in, F_out = (4096, 128, 128)
        h = jax.random.normal(k1, (N, F_in), dtype=jnp.float32)
        adj = jax.random.randint(k2, (N, N), 0, 2).astype(jnp.float32)
        W = jax.random.normal(k3, (F_in, F_out), dtype=jnp.float32) * (1.414 / np.sqrt(F_in))
        a = jax.random.normal(k4, (2 * F_out, 1), dtype=jnp.float32) * (1.414 / np.sqrt(2 * F_out))
        return {'h': h, 'adj': adj, 'W': W, 'a': a}
    _L0_gnn_all = _L0_gnn_setup()
    _L0_gnn_in = {k: v for k, v in _L0_gnn_all.items() if k in ('W', 'a')}
    del _L0_gnn_all

    def _L1_gnn_setup():
        import jax, jax.numpy as jnp
        import numpy as np
        N = 4096
        D_IN = 128
        D_OUT = 128
        key = jax.random.key(seed)
        k1, k2, k3 = jax.random.split(key, 3)
        input = jax.random.normal(k1, (N, D_IN), dtype=jnp.float32)
        adjacencyMatrix = jax.random.uniform(k2, (N, N), dtype=jnp.float32)
        W = jax.random.normal(k3, (D_OUT, D_IN), dtype=jnp.float32) * (1.0 / np.sqrt(D_IN))
        return {'input': input, 'adjacencyMatrix': adjacencyMatrix, 'W': W}
    _L1_gnn_all = _L1_gnn_setup()
    _L1_gnn_in = {k: v for k, v in _L1_gnn_all.items() if k in ('W',)}
    del _L1_gnn_all
    return {'x': x, 'adj': adj, 'L0_gnn_W': _L0_gnn_in['W'], 'L0_gnn_a': _L0_gnn_in['a'], 'L1_gnn_W': _L1_gnn_in['W']}

def reference(x, adj, L0_gnn_W, L0_gnn_a, L1_gnn_W):
    import jax
    import jax.numpy as jnp

    def _L0_gnn_ref(h, adj, W, a):
        import jax, jax.numpy as jnp
        import numpy as np
        NEG_BIG = -9000000000000000.0
        ALPHA = 0.2
        F_out = W.shape[1]
        Wh = h @ W
        a1 = a[:F_out, 0]
        a2 = a[F_out:, 0]
        s1 = Wh @ a1
        s2 = Wh @ a2
        e = jax.nn.leaky_relu(s1[:, None] + s2[None, :], negative_slope=ALPHA)
        e = jnp.where(adj > 0, e, NEG_BIG)
        attention = jax.nn.softmax(e, axis=1)
        h_prime = attention @ Wh
        return jax.nn.elu(h_prime)

    def _L1_gnn_ref(input, adjacencyMatrix, W):
        import jax, jax.numpy as jnp
        import numpy as np
        N = 4096
        D_IN = 128
        D_OUT = 128
        d_inv_sqrt = jnp.sum(adjacencyMatrix, axis=1) ** (-0.5)
        A_norm = adjacencyMatrix * d_inv_sqrt[:, None] * d_inv_sqrt[None, :]
        h = A_norm @ input
        return h @ W.T
    x = _layernorm(x + _L0_gnn_ref(x, adj, L0_gnn_W, L0_gnn_a), axis=-1)
    x = _layernorm(x + _L1_gnn_ref(x, adj, L1_gnn_W), axis=-1)
    return x

_drawn_inputs = setup_inputs


def setup_inputs(seed=0):
    import zlib

    import numpy as np

    out = dict(_drawn_inputs(seed))
    spreads = {}
    factors = {}
    for name, (base, spread) in spreads.items():
        noise = np.random.default_rng([zlib.crc32(name.encode()), seed]).standard_normal(out[name].shape)
        drawn = base * np.exp(spread * noise) if base else spread * noise
        out[name] = jnp.asarray(drawn.astype(out[name].dtype))
    for name, factor in factors.items():
        out[name] = (out[name] * factor).astype(out[name].dtype)
    return out
```

```python
from contextlib import ExitStack

import numpy as np
import concourse.bass as bass
from concourse import mybir

ALU = mybir.AluOpType
ACT = mybir.ActivationFunctionType
F32 = mybir.dt.float32
BF16 = mybir.dt.bfloat16
FP8 = mybir.dt.float8e4
U8 = mybir.dt.uint8
I32 = mybir.dt.int32
AX_X = mybir.AxisListType.X

P = 128
SUPER = 512
TILES = SUPER // P
COLS = 1024
SLOTS = 2
BANKS = 4
RING = 4
AHEAD = 2
PARTS = 3
LATE_BUFS = 4
SLOPE = 0.2
EPS = 1e-5
SPREAD = 80.0


def build_common(nc, x, adj, w_gat, a_gat, w_gcn, ident, ident16, out, flag):
    N, F = x.shape
    U = N // SUPER
    JB = N // P
    CH = N // COLS
    PPC = COLS // P // 2
    PAIRS = JB // 2
    STEPS = U * JB
    FE = F + 2
    EARLY = PAIRS // 2
    LATE = PAIRS - EARLY
    assert LATE % LATE_BUFS == 0 and LATE // LATE_BUFS == TILES // 2
    assert PPC == TILES and PAIRS % BANKS == 0 and JB % RING == 0

    r_dram = nc.dram_tensor("r_scratch", (N,), F32, kind="Internal").ap()
    x1_dram = nc.dram_tensor("x1_scratch", (P, JB * F), F32, kind="Internal").ap()
    y_dram = nc.dram_tensor("y_scratch", (P, JB * PARTS * F), BF16, kind="Internal").ap()

    with ExitStack() as ctx:
        def sb(name, shape, dt=F32):
            return ctx.enter_context(nc.sbuf_tensor(name, shape, dt))

        def ps(name, shape):
            return ctx.enter_context(nc.psum_tensor(name, shape, F32))

        def sem(name):
            return ctx.enter_context(nc.semaphore(name))

        adjT = sb("adjT", [P, JB * N], FP8)
        chunk = sb("chunk", [P, SLOTS, TILES, COLS])
        feat = sb("feat", [P, JB, FE])
        blk = sb("blk", [P, RING, SUPER])
        r_row = sb("r_row", [P, 2, SUPER])
        h = sb("h", [P, TILES, F])
        he = sb("he", [P, TILES, F])
        xt = sb("xt", [P, TILES, F])
        x1 = sb("x1", [P, TILES, F])
        yp = sb("yp", [P, TILES, PARTS, F], BF16)
        deg_junk = sb("deg_junk", [P, 2, COLS], U8)
        chk_junk = sb("chk_junk", [P, 2, COLS], U8)
        eye = sb("eye", [P, P])
        eye16 = sb("eye16", [P, P], BF16)
        w1T = sb("w1T", [P, P])
        ones = sb("ones", [2, P])
        ones_col = sb("ones_col", [P, 1])
        smax = sb("smax", [P, 4])
        smax1 = sb("smax1", [2, 4])
        s_col = sb("s_col", [P, 2, JB])
        q_col = sb("q_col", [P, JB])
        g_col = sb("g_col", [P, JB])
        bad = sb("bad", [P, U * PAIRS + 1])
        badc = sb("badc", [P, 1])
        dpart = sb("dpart", [P, 2, TILES, CH])
        dsum = sb("dsum", [P, TILES])
        dinv = sb("dinv", [P, JB])
        mhalf = sb("mhalf", [P, TILES])
        rden = sb("rden", [P, TILES])
        stats = sb("stats", [P, TILES, 6])
        mv = sb("mv", [P, TILES, 2])
        vpe = sb("vpe", [P, TILES])
        rstd = sb("rstd", [P, TILES])

        tb = ps("tb", [P, BANKS, SUPER])
        acc = ps("acc", [P, 4, SUPER])

        early = adjT[:].bitcast(F32)
        x_sb = early[:, 0:JB * F].rearrange("p (t f) -> p t f", f=F)
        xT = early[:, JB * F:2 * JB * F].rearrange("p (t f) -> p t f", f=F)
        w0 = early[:, 2 * JB * F:2 * JB * F + FE]
        w0T = early[:, 2 * JB * F + 256:2 * JB * F + 384]
        w1 = early[:, 2 * JB * F + 384:2 * JB * F + 512]
        a_sb = early[:, 2 * JB * F + 512:2 * JB * F + 514]
        r_col = early[:, 2 * JB * F + 520:2 * JB * F + 520 + JB]
        rT = early[0:JB, 2 * JB * F + 640:2 * JB * F + 768]
        y_half = [chunk[:, s].rearrange("p a c -> p (a c)").bitcast(BF16)[:, 0:JB // 2 * PARTS * F]
                  .rearrange("p (t k f) -> p t k f", k=PARTS, f=F) for s in range(SLOTS)]
        x1_back = feat[:].rearrange("p t f -> p (t f)")[:, 0:2 * SUPER].rearrange("p (b a f) -> p b a f", b=2, f=F)
        late = [feat[:].rearrange("p t f -> p (t f)")[:, (2 + n) * SUPER:(2 + n) * SUPER + COLS] for n in (0, 2, 4)]
        late.append(chunk[:, 0].rearrange("p a c -> p (a c)")[:, (TILES - 1) * COLS:TILES * COLS])
        adjT_v = adjT[:].rearrange("p (t i) -> p t i", i=N)
        adj_hi = chunk[:].bitcast(BF16).rearrange("p s a (c w) -> p s a c w", w=2)[:, :, :, :, 1]
        tb16 = tb[:].bitcast(BF16)

        chunk_in = [sem(f"chunk_in{i}") for i in range(SLOTS)]
        r_in = [sem(f"r_in{i}") for i in range(2)]
        y_in = [sem(f"y_in{i}") for i in range(3)]
        x1_in = [sem(f"x1_in{i}") for i in range(2)]
        out_st = [sem(f"out_st{i}") for i in range(2)]
        late_in = [sem(f"late_in{i}") for i in range(LATE_BUFS)]
        x_in = sem("x_in")
        xt_in = sem("xt_in")
        w_in = sem("w_in")
        const_set = sem("const_set")
        xT_ready = sem("xT_ready")
        xT_act = sem("xT_act")
        xT_dve = sem("xT_dve")
        wT_ready = sem("wT_ready")
        wT_sb = sem("wT_sb")
        wa_ready = sem("wa_ready")
        wa_sb = sem("wa_sb")
        feat_ready = sem("feat_ready")
        feat_act = sem("feat_act")
        feat_dve = sem("feat_dve")
        smax_col = sem("smax_col")
        smax_T = sem("smax_T")
        smax_one = sem("smax_one")
        smax_bc = sem("smax_bc")
        smax_sb = sem("smax_sb")
        s_prep = sem("s_prep")
        exps = sem("exps")
        rT_ready = sem("rT_ready")
        rT_sb = sem("rT_sb")
        r_stored = sem("r_stored")
        feat_scaled = sem("feat_scaled")

        t_ready = sem("t_ready")
        p_made = sem("p_made")
        kept = sem("kept")
        mm_done = sem("mm_done")
        summed = sem("summed")
        checked = sem("checked")
        late_checked = sem("late_checked")
        den_rec = sem("den_rec")
        acc_read = sem("acc_read")
        neg_made = sem("neg_made")
        elu_exp = sem("elu_exp")
        elu_sum = sem("elu_sum")
        res_ready = sem("res_ready")
        dsum_ready = sem("dsum_ready")
        dinv_ready = sem("dinv_ready")
        stat_ready = sem("stat_ready")
        mv_ready = sem("mv_ready")
        var_ready = sem("var_ready")
        rstd_ready = sem("rstd_ready")
        x1_ready = sem("x1_ready")
        y_ready = sem("y_ready")
        split = sem("split")
        x1_st = sem("x1_st")
        y_st = sem("y_st")
        conv_done = sem("conv_done")
        hT_sb = sem("hT_sb")
        z_ready = sem("z_ready")
        o_ready = sem("o_ready")
        bad_ready = sem("bad_ready")
        bad_sum = sem("bad_sum")
        flag_set = sem("flag_set")

        x_v = x.rearrange("(t p) f -> p t f", p=P)
        adj_v = adj.rearrange("(u a p) c -> u p a c", a=TILES, p=P)
        out_v = out.rearrange("(u a p) f -> u p a f", a=TILES, p=P)

        def at(v, u):
            return v[u] if isinstance(u, int) else v[bass.ds(u, 1)].rearrange("o p a f -> (o p) a f")

        def acc0(par):
            return acc[:, 2 * par:2 * par + 2, 0:2 * (F + 1)].rearrange("p b (a f) -> p b a f", a=2)

        block = ctx.enter_context(nc.Block())

        @block.sync
        def _(sp):
            def load(u, c):
                sp.dma_start(chunk[:, c % SLOTS], at(adj_v, u)[:, :, c * COLS:(c + 1) * COLS]
                             ).then_inc(chunk_in[c % SLOTS], 16)

            def freed(u, c):
                n = (u * CH + c - SLOTS + 1) * PPC
                sp.wait_ge(t_ready, n)
                sp.wait_ge(summed, n)
                sp.wait_ge(checked, n)

            def load_r(u, par):
                sp.dma_start(r_row[:, par], r_dram[bass.ds(u * SUPER, SUPER)].partition_broadcast(P)
                             ).then_inc(r_in[par], 16)

            def load_xt(w):
                sp.dma_start(xt[:], x_v[:, bass.ds(w * TILES, TILES), :]).then_inc(xt_in, 16)

            sp.dma_start(w0[:, 0:F], w_gat).then_inc(w_in, 16)
            sp.dma_start(eye[:], ident).then_inc(w_in, 16)
            sp.dma_start(w1, w_gcn).then_inc(w_in, 16)
            with nc.allow_non_contiguous_dma(reason="the attention vector is tiny"):
                sp.dma_start(a_sb, a_gat.rearrange("(k p) o -> p (k o)", p=P)).then_inc(w_in, 16)
            sp.dma_start(eye16[:], ident16).then_inc(w_in, 16)
            sp.dma_start(x_sb, x_v).then_inc(x_in, 16)
            load(0, 0)
            load(0, 1)
            sp.wait_ge(r_stored, 16)
            load_r(0, 0)
            for c in range(SLOTS, CH):
                freed(0, c)
                load(0, c)

            def super_loads(u, par, first=False):
                for c in range(CH):
                    freed(u, c)
                    load(u, c)
                    if c == 0:
                        sp.wait_ge(p_made, (u - 1) * JB)
                        load_r(u, par)
                    if c == 1:
                        if not first:
                            sp.wait_ge(res_ready, u - 1)
                        load_xt(u - 1)

            super_loads(1, 1, first=True)
            with sp.Fori(1, U // 2) as pair:
                super_loads(pair * 2, 0)
                super_loads(pair * 2 + 1, 1)
            sp.wait_ge(res_ready, U - 1)
            load_xt(U - 1)

            half = JB // 2
            for n, (s, lo, hi) in enumerate([(0, 0, half), (1, 0, half - TILES), (1, half - TILES, half)]):
                freed(U, s)
                sp.wait_ge(y_st, 16 * ((s * half + hi) // TILES))
                cols = slice((s * half + lo) * PARTS * F, (s * half + hi) * PARTS * F)
                sp.dma_start(y_half[s][:, lo:hi].rearrange("p t k f -> p (t k f)"), y_dram[:, cols]
                             ).then_inc(y_in[n], 16)

            def load_x1(w, par):
                sp.dma_start(x1_back[:, par].rearrange("p a f -> p (a f)"),
                             x1_dram[:, bass.ds(w * SUPER, SUPER)]).then_inc(x1_in[par], 16)

            def load_late(w, k):
                a, c = 2 * (k // CH) + 1, k % CH
                sp.dma_start(late[k % LATE_BUFS], at(adj_v, w)[:, a, c * COLS:(c + 1) * COLS]
                             ).then_inc(late_in[k % LATE_BUFS], 16)

            def load_late_rest(w, ks):
                for k in ks:
                    sp.wait_ge(late_checked, w * LATE + k - LATE_BUFS + 1)
                    load_late(w, k)

            sp.wait_ge(mm_done, STEPS)
            sp.wait_ge(x1_st, 16 * U)
            load_x1(0, 0)
            load_x1(1, 1)
            for k in range(LATE_BUFS):
                load_late(0, k)
            load_late_rest(0, range(LATE_BUFS, LATE))
            load_late_rest(1, range(LATE))
            with sp.Fori(1, U // 2) as pair:
                for par in range(2):
                    w = pair * 2 + par
                    load_late_rest(w, range(LATE_BUFS))
                    sp.wait_ge(res_ready, U + w - 1)
                    load_x1(w, par)
                    load_late_rest(w, range(LATE_BUFS, LATE))

        @block.tensor
        def _(pe):
            pe.wait_ge(w_in, 80)
            pe.transpose(tb[:, 0, 0:P], w0[:, 0:F], eye[:])
            pe.transpose(tb[:, 0, P:2 * P], w1, eye[:]).then_inc(wT_ready, 1)
            pe.wait_ge(wT_sb, 1)
            pe.matmul(tb[:, 1, 0:2], w0T, a_sb, start=True, stop=True).then_inc(wa_ready, 1)
            pe.wait_ge(wa_sb, 1)
            pe.wait_ge(x_in, 16)
            for g in range(U):
                if g >= BANKS:
                    pe.wait_ge(xT_act if g % 2 == 0 else xT_dve, (g - BANKS) // 2 + 1)
                for a in range(TILES):
                    last = pe.transpose(tb[:, g % BANKS, a * P:(a + 1) * P], x_sb[:, g * TILES + a, :], eye[:])
                last.then_inc(xT_ready, 1)
            for t in range(JB):
                g, b = t // TILES, (t // 2) % 4
                if t % TILES == 0:
                    pe.wait_ge(xT_act if g % 2 == 0 else xT_dve, g // 2 + 1)
                if t >= 8 and t % 2 == 0:
                    n = (t - 8) // 2
                    pe.wait_ge(feat_act if n % 2 == 0 else feat_dve, n // 2 + 1)
                o = (t % 2) * FE
                last = pe.matmul(acc[:, b, o:o + FE], xT[:, t, :], w0, start=(t % 2 == 0), stop=True,
                                 skip_group_check=True)
                if t % 2:
                    last.then_inc(feat_ready, 1)
            pe.wait_ge(smax_col, 2)
            pe.transpose(tb[0:2, 0, 0:P], smax[:, 0:2], eye[:]).then_inc(smax_T, 1)
            pe.wait_ge(smax_one, 2)
            pe.matmul(tb[:, 1, 0:2], ones[:], smax1[:, 2:4], start=True, stop=True).then_inc(smax_bc, 1)
            pe.wait_ge(exps, 1)
            pe.transpose(tb[0:JB, 2, 0:P], r_col, eye[:]).then_inc(rT_ready, 1)
            pe.wait_ge(rT_sb, 1)

            def transposes(u, m):
                c = (m // PPC) % CH
                if m % PPC == 0:
                    pe.wait_ge(chunk_in[c % SLOTS], 16 * (u * (CH // SLOTS) + m // PPC // SLOTS + 1))
                for half in range(2):
                    col = (m % PPC * 2 + half) * P
                    for a in range(TILES):
                        o = half * SUPER + a * P
                        last = pe.transpose(tb16[:, m % BANKS, o:o + P], adj_hi[:, c % SLOTS, a, col:col + P],
                                            eye16[:])
                last.then_inc(t_ready, 1)

            def attend(u, par, last_super=False):
                sums = acc0(par)
                for m in range(PAIRS):
                    if not (last_super and m + AHEAD >= PAIRS):
                        if not (isinstance(u, int) and u == 0 and m + AHEAD < BANKS):
                            pe.wait_ge(kept, u * PAIRS + m + AHEAD - BANKS + 1)
                        transposes(u, m + AHEAD)
                    for k in (2 * m, 2 * m + 1):
                        pe.wait_ge(p_made, u * JB + k + 1)
                        for a in range(TILES):
                            last = pe.matmul(sums[:, a // 2, a % 2, :], blk[:, k % RING, a * P:(a + 1) * P],
                                             feat[:, k, 0:F + 1], start=(k == 0 and a % 2 == 0),
                                             stop=(k == JB - 1), skip_group_check=True)
                        last.then_inc(mm_done, 1)
                pe.wait_ge(acc_read, u)

            for m in range(AHEAD):
                transposes(0, m)
            pe.wait_ge(feat_scaled, 1)
            attend(0, 0)
            attend(1, 1)
            with pe.Fori(1, U // 2 - 1) as pair:
                attend(pair * 2, 0)
                attend(pair * 2 + 1, 1)
            attend(U - 2, 0)
            attend(U - 1, 1, last_super=True)

            def convolve(u, par):
                pe.wait_ge(kept, (u + 1) * PAIRS)
                if u >= 2:
                    pe.wait_ge(hT_sb, u - 1)
                for t in range(JB):
                    if u == 0 and t in (0, JB // 2, JB - TILES):
                        pe.wait_ge(y_in[(0, JB // 2, JB - TILES).index(t)], 16)
                    for part in range(PARTS):
                        last = pe.matmul(acc[:, par, :], y_half[t // (JB // 2)][:, t % (JB // 2), part, :],
                                         adjT_v[:, t, u * SUPER:(u + 1) * SUPER],
                                         start=(t == 0 and part == 0), stop=(t == JB - 1 and part == PARTS - 1))
                last.then_inc(conv_done, 1)

            def project(w, par):
                pe.wait_ge(hT_sb, w + 1)
                if w >= 2:
                    pe.wait_ge(res_ready, U + w - 1)
                for a in range(TILES):
                    last = pe.matmul(tb[:, par, a * F:(a + 1) * F], blk[:, par, a * P:(a + 1) * P], w1T[:],
                                     start=(a == 0), stop=True, skip_group_check=True)
                last.then_inc(z_ready, 1)

            for u in range(U):
                convolve(u, u % 2)
                if u == 0:
                    pe.wait_ge(kept, U * PAIRS)
                else:
                    project(u - 1, (u - 1) % 2)
            pe.wait_ge(bad_ready, 1)
            pe.matmul(tb[0:1, 2, 0:1], badc[:], ones_col[:], start=True, stop=True).then_inc(bad_sum, 1)
            project(U - 1, (U - 1) % 2)

        @block.scalar
        def _(act):
            for g in range(0, U, 2):
                act.wait_ge(xT_ready, g + 1)
                act.copy(xT[:, g * TILES:(g + 1) * TILES, :],
                         tb[:, g % BANKS, :].rearrange("p (a n) -> p a n", a=TILES)).then_inc(xT_act, 1)
            for n in range(0, JB // 2, 2):
                act.wait_ge(feat_ready, n + 1)
                act.copy(feat[:, 2 * n:2 * n + 2, :], acc[:, n % 4, 0:2 * FE].rearrange("p (a n) -> p a n", a=2)
                         ).then_inc(feat_act, 1)
            act.wait_ge(s_prep, 2)
            act.activation(r_col, s_col[:, 0, :], ACT.Exp, scale=-(1.0 - SLOPE)).then_inc(exps, 1)
            act.activation(q_col[:], s_col[:, 1, :], ACT.Exp, scale=1.0 - SLOPE).then_inc(exps, 1)
            act.activation(g_col[:], s_col[:, 1, :], ACT.Exp, scale=SLOPE).then_inc(exps, 1)
            act.wait_ge(rT_ready, 1)
            act.copy(rT, tb[0:JB, 2, 0:P]).then_inc(rT_sb, 1)
            act.wait_ge(rT_sb, 1)
            act.dma_start(r_dram.rearrange("(t p) -> t p", p=P), rT).then_inc(r_stored, 16)
            act.wait_ge(r_stored, 16)

            def row_sum(n):
                g, a = n // TILES, n % TILES
                u, c = g // CH, g % CH
                if a == 0:
                    act.wait_ge(chunk_in[c % SLOTS], 16 * (g // SLOTS + 1))
                if n >= 2:
                    act.wait_ge(summed, n - 1)
                if u >= 2 and c == 0 and a == 0:
                    act.wait_ge(dsum_ready, u - 1)
                act.activation(deg_junk[:, n % 2, :], chunk[:, c % SLOTS, a, :], ACT.Copy,
                               accum_out=dpart[:, u % 2, a, c:c + 1]).then_inc(summed, 1)

            def keep(u, m):
                act.wait_ge(p_made, u * JB + 2 * m + 2)
                act.copy(adjT_v[:, 2 * m:2 * m + 2, u * SUPER:(u + 1) * SUPER],
                         tb16[:, m % BANKS, :].rearrange("p (t i) -> p t i", t=2), saturate=False
                         ).then_inc(kept, 1)

            def weigh(w):
                par = w % 2
                act.wait_ge(den_rec, w + 1)
                if w >= 1:
                    act.wait_ge(x1_ready, w)
                    act.wait_ge(split, 5 * w)
                for a in range(TILES):
                    last = act.activation(h[:, a, :], acc0(par)[:, a // 2, a % 2, 0:F], ACT.Copy,
                                          scale=rden[:, a:a + 1])
                last.then_inc(acc_read, 1)
                act.wait_ge(acc_read, w + 1)
                act.activation(he[:], h[:], ACT.Relu, scale=-1.0).then_inc(neg_made, 1)
                act.wait_ge(neg_made, w + 1)
                act.activation(he[:], he[:], ACT.Exp, scale=-1.0).then_inc(elu_exp, 1)

            def scale_y(w):
                act.wait_ge(x1_ready, w + 1)
                act.wait_ge(dinv_ready, w + 1)
                for a in range(TILES):
                    t = w * TILES + a
                    last = act.activation(he[:, a, :], x1[:, a, :], ACT.Copy, scale=dinv[:, t:t + 1])
                last.then_inc(y_ready, 1)

            for n in range(AHEAD):
                row_sum(n)
            for u in range(U):
                for m in range(PAIRS):
                    keep(u, m)
                    if u * PAIRS + m + AHEAD < U * PAIRS:
                        row_sum(u * PAIRS + m + AHEAD)
                    if u >= 1 and m == 2:
                        weigh(u - 1)
                    if u >= 1 and m == 9:
                        scale_y(u - 1)
            weigh(U - 1)
            scale_y(U - 1)

            def copy_hT(w, par):
                act.wait_ge(conv_done, w + 1)
                act.copy(blk[:, par, :], acc[:, par, :]).then_inc(hT_sb, 1)

            def store(w, par):
                act.wait_ge(o_ready, w + 1)
                act.dma_start(at(out_v, w), blk[:, 2 + par, :].rearrange("p (a f) -> p a f", f=F)
                              ).then_inc(out_st[par], 16)

            copy_hT(0, 0)
            copy_hT(1, 1)
            with act.Fori(1, U // 2) as pair:
                for par in range(2):
                    w = pair * 2 + par
                    act.wait_ge(z_ready, w - 1)
                    copy_hT(w, par)
                    store(w - 2, par)
            store(U - 2, 0)
            store(U - 1, 1)
            act.wait_ge(out_st[0], 16 * (U // 2))
            act.wait_ge(out_st[1], 16 * (U // 2))

        @block.gpsimd
        def _(pool):
            def root(n, dst, src, ready, done):
                pool.wait_ge(ready, n + 1)
                pool.tensor_tensor(dst, src, mhalf[:], ALU.pow).then_inc(done, 1)

            def parts(w):
                pool.wait_ge(y_ready, w + 1)
                pool.wait_ge(y_st, 16 * w)
                for part in range(PARTS):
                    pool.tensor_copy(yp[:, :, part, :], he[:]).then_inc(split, 1)
                    pool.wait_ge(split, w * 5 + 2 * part + 1)
                    if part < PARTS - 1:
                        pool.tensor_tensor(he[:], he[:], yp[:, :, part, :], ALU.subtract).then_inc(split, 1)
                        pool.wait_ge(split, w * 5 + 2 * part + 2)
                pool.dma_start(y_dram[:, w * SUPER * PARTS:(w + 1) * SUPER * PARTS],
                               yp[:].rearrange("p a k f -> p (a k f)")).then_inc(y_st, 16)
                pool.dma_start(x1_dram[:, w * SUPER:(w + 1) * SUPER],
                               x1[:].rearrange("p a f -> p (a f)")).then_inc(x1_st, 16)

            pool.wait_ge(const_set, 4)
            for w in range(U):
                root(w, dinv[:, w * TILES:(w + 1) * TILES], dsum[:], dsum_ready, dinv_ready)
                root(w, rstd[:], vpe[:], var_ready, rstd_ready)
                parts(w)
            for w in range(U):
                root(U + w, rstd[:], vpe[:], var_ready, rstd_ready)
            pool.wait_ge(y_st, 16 * U)
            pool.wait_ge(x1_st, 16 * U)

        @block.vector
        def _(dve):
            dve.memset(ones[:], 1.0).then_inc(const_set, 1)
            dve.memset(mhalf[:], -0.5).then_inc(const_set, 1)
            dve.memset(ones_col[:], 1.0).then_inc(const_set, 1)
            dve.memset(bad[:], 0.0).then_inc(const_set, 1)
            dve.wait_ge(wT_ready, 1)
            dve.tensor_copy(w0T, tb[:, 0, 0:P]).then_inc(wT_sb, 1)
            dve.tensor_copy(w1T[:], tb[:, 0, P:2 * P]).then_inc(wT_sb, 1)
            dve.wait_ge(wa_ready, 1)
            dve.tensor_copy(w0[:, F:FE], tb[:, 1, 0:2]).then_inc(wa_sb, 1)
            for g in range(1, U, 2):
                dve.wait_ge(xT_ready, g + 1)
                dve.tensor_copy(xT[:, g * TILES:(g + 1) * TILES, :],
                                tb[:, g % BANKS, :].rearrange("p (a n) -> p a n", a=TILES)).then_inc(xT_dve, 1)
            for n in range(1, JB // 2, 2):
                dve.wait_ge(feat_ready, n + 1)
                dve.tensor_copy(feat[:, 2 * n:2 * n + 2, :],
                                acc[:, n % 4, 0:2 * FE].rearrange("p (a n) -> p a n", a=2)).then_inc(feat_dve, 1)
            dve.wait_ge(feat_act, JB // 4)
            dve.wait_ge(feat_dve, JB // 4)
            dve.tensor_reduce(smax[:, 0:1], feat[:, :, F + 1], AX_X, ALU.max).then_inc(smax_col, 1)
            dve.tensor_reduce(smax[:, 1:2], feat[:, :, F + 1], AX_X, ALU.min, negate=True).then_inc(smax_col, 1)
            dve.wait_ge(smax_T, 1)
            dve.tensor_reduce(smax1[:, 0:1], tb[0:2, 0, 0:P], AX_X, ALU.max).then_inc(smax_one, 1)
            dve.wait_ge(smax_one, 1)
            dve.wait_ge(w_in, 80)
            dve.tensor_scalar(smax1[:, 2:4], eye[0:2, 0:2], smax1[:, 0:1], None, ALU.mult).then_inc(smax_one, 1)
            dve.wait_ge(smax_bc, 1)
            dve.tensor_copy(smax[:, 2:4], tb[:, 1, 0:2]).then_inc(smax_sb, 1)
            dve.wait_ge(smax_sb, 1)
            dve.tensor_scalar(s_col[:, 0, :], feat[:, :, F], smax[:, 2:3], 0.0, ALU.add, ALU.max).then_inc(s_prep, 1)
            dve.tensor_scalar(s_col[:, 1, :], feat[:, :, F + 1], smax[:, 2:3], -SPREAD, ALU.subtract, ALU.max
                              ).then_inc(s_prep, 1)
            dve.wait_ge(const_set, 4)
            dve.tensor_scalar(bad[:, U * PAIRS:], smax[:, 2:3], smax[:, 3:4], SPREAD, ALU.add, ALU.is_gt
                              ).then_inc(s_prep, 1)
            dve.wait_ge(s_prep, 3)
            dve.memset(feat[:, :, F:F + 1], 1.0).then_inc(s_prep, 1)
            dve.wait_ge(s_prep, 4)
            dve.wait_ge(exps, 3)
            dve.tensor_tensor(feat[:, :, 0:F + 1], feat[:, :, 0:F + 1],
                              g_col[:].rearrange("p (t o) -> p t o", o=1).to_broadcast([P, JB, F + 1]), ALU.mult
                              ).then_inc(feat_scaled, 1)

            def count_bad(piece, n, junk):
                return dve.scalar_tensor_tensor(chk_junk[:, junk, :], piece, 1.0, piece, ALU.not_equal,
                                                ALU.logical_and, accum_out=bad[:, bass.ds(n, 1)])

            def check(u, m):
                n = u * EARLY + m // 2
                c, a = (m // TILES) % CH, m % TILES
                if a == 0:
                    dve.wait_ge(chunk_in[c % SLOTS], 16 * (u * (CH // SLOTS) + m // TILES // SLOTS + 1))
                if not (isinstance(n, int) and n < 2):
                    dve.wait_ge(checked, n * 2 - 2)
                count_bad(chunk[:, c % SLOTS, a, :], n, m // 2 % 2).then_inc(checked, 2)

            def late_checks(w):
                for k in range(LATE):
                    n = w * LATE + k
                    if k % LATE_BUFS == k:
                        dve.wait_ge(late_in[k % LATE_BUFS], w * 32 + 16)
                    else:
                        dve.wait_ge(late_in[k % LATE_BUFS], w * 32 + 32)
                    if not (isinstance(n, int) and n < 2):
                        dve.wait_ge(late_checked, n - 1)
                    count_bad(late[k % LATE_BUFS], n + U * EARLY, k % 2).then_inc(late_checked, 1)

            def weights(u, k, par):
                if k == 0:
                    dve.wait_ge(r_in[par], (u - par) * 8 + 16)
                if k % 2 == 0:
                    dve.wait_ge(t_ready, u * PAIRS + k // 2 + 1)
                if not (isinstance(u, int) and u == 0 and k < RING):
                    dve.wait_ge(mm_done, u * JB + k + 1 - RING)
                m = k // 2
                dve.scalar_tensor_tensor(blk[:, k % RING, :], r_row[:, par, :], q_col[:, k:k + 1],
                                         tb16[:, m % BANKS, k % 2 * SUPER:(k % 2 + 1) * SUPER],
                                         ALU.max, ALU.mult).then_inc(p_made, 1)

            def attend(u, par, prev=True, last_super=False):
                for m in range(PAIRS):
                    weights(u, 2 * m, par)
                    weights(u, 2 * m + 1, par)
                    if m % 2 == 0 and not (last_super and m + AHEAD >= PAIRS):
                        check(u, m + AHEAD)
                    if prev:
                        w, wp = u - 1, 1 - par
                        if m == 1:
                            denominators(w, wp)
                        if m == 2:
                            degrees(w, wp)
                        if m == 5:
                            residual(w)
                        if m == 6:
                            moments(w)
                        if m == 8:
                            layer0_out(w)

            def denominators(w, par):
                dve.wait_ge(mm_done, (w + 1) * JB)
                dve.wait_ge(acc_read, w)
                dve.reciprocal(rden[:].rearrange("p (b a) -> p b a", a=2), acc0(par)[:, :, :, F]).then_inc(den_rec, 1)

            def degrees(w, par):
                dve.wait_ge(summed, (w + 1) * PAIRS)
                dve.wait_ge(dinv_ready, w)
                dve.tensor_reduce(dsum[:], dpart[:, par], AX_X, ALU.add).then_inc(dsum_ready, 1)

            def residual(w):
                dve.wait_ge(elu_exp, w + 1)
                dve.scalar_tensor_tensor(h[:], h[:], 0.0, he[:], ALU.max, ALU.add).then_inc(elu_sum, 1)
                dve.wait_ge(elu_sum, w + 1)
                dve.wait_ge(xt_in, w * 16 + 16)
                dve.scalar_tensor_tensor(h[:], h[:], -1.0, xt[:], ALU.add, ALU.add).then_inc(res_ready, 1)

            def moments(n):
                dve.wait_ge(res_ready, n + 1)
                for a in range(TILES):
                    last = dve.bn_stats(stats[:, a, :], h[:, a, :])
                last.then_inc(stat_ready, 1)
                dve.wait_ge(const_set, 4)
                dve.wait_ge(stat_ready, n + 1)
                for a in range(TILES):
                    last = dve.bn_aggr(mv[:, a, :], stats[:, a, :])
                last.then_inc(mv_ready, 1)
                dve.wait_ge(mv_ready, n + 1)
                dve.tensor_scalar(vpe[:], mv[:, :, 1], EPS, None, ALU.add).then_inc(var_ready, 1)

            def layer0_out(w):
                dve.wait_ge(rstd_ready, w + 1)
                if not isinstance(w, int) or w >= 1:
                    dve.wait_ge(x1_st, w * 16)
                    dve.wait_ge(y_ready, w)
                for a in range(TILES):
                    last = dve.tensor_scalar(x1[:, a, :], h[:, a, :], mv[:, a, 0:1], rstd[:, a:a + 1],
                                             ALU.subtract, ALU.mult)
                last.then_inc(x1_ready, 1)

            for m in range(0, AHEAD, 2):
                check(0, m)
            attend(0, 0, prev=False)
            attend(1, 1)
            with dve.Fori(1, U // 2 - 1) as pair:
                attend(pair * 2, 0)
                attend(pair * 2 + 1, 1)
            attend(U - 2, 0)
            attend(U - 1, 1, last_super=True)
            w = U - 1
            denominators(w, 1)
            degrees(w, 1)
            residual(w)
            moments(w)
            layer0_out(w)
            dve.wait_ge(checked, U * PAIRS)

            def layer1_res(w, par):
                if isinstance(w, int) and w == 0:
                    dve.wait_ge(x1_ready, U)
                else:
                    dve.wait_ge(o_ready, w)
                dve.wait_ge(z_ready, w + 1)
                dve.wait_ge(x1_in[par], (w - par) * 8 + 16)
                for a in range(TILES):
                    last = dve.scalar_tensor_tensor(
                        h[:, a, :], tb[:, par, a * F:(a + 1) * F], dinv[:, bass.ds(w * TILES + a, 1)],
                        x1_back[:, par, a, :], ALU.mult, ALU.add)
                last.then_inc(res_ready, 1)

            def layer1_out(w, par, stored):
                if stored is not None:
                    dve.wait_ge(out_st[par], stored)
                dve.wait_ge(rstd_ready, U + w + 1)
                for a in range(TILES):
                    last = dve.tensor_scalar(blk[:, 2 + par, a * F:(a + 1) * F], h[:, a, :], mv[:, a, 0:1],
                                             rstd[:, a:a + 1], ALU.subtract, ALU.mult)
                last.then_inc(o_ready, 1)

            late_checks(0)
            for w in range(2):
                late_checks(w + 1)
                layer1_res(w, w)
                moments(U + w)
                layer1_out(w, w, None)
            with dve.Fori(1, U // 2 - 1) as pair:
                for par in range(2):
                    w = pair * 2 + par
                    late_checks(w + 1)
                    layer1_res(w, par)
                    moments(w + U)
                    layer1_out(w, par, (w - par) * 8)
            late_checks(U - 1)
            dve.wait_ge(late_checked, U * LATE)
            dve.tensor_reduce(badc[:], bad[:], AX_X, ALU.add).then_inc(bad_ready, 1)
            for w in (U - 2, U - 1):
                layer1_res(w, w % 2)
                moments(w + U)
                layer1_out(w, w % 2, (U - 2) * 8)
            dve.wait_ge(bad_sum, 1)
            dve.tensor_scalar(flag[:], tb[0:1, 2, 0:1], 0.0, None, ALU.is_gt).then_inc(flag_set, 1)


def build_general(nc, x, adj, w_gat, a_gat, w_gcn, ident, out, flag):
    N, F = x.shape
    T = N // P
    G = SUPER // P
    GROUPS = T // G
    FE = F + 2
    NEG = 9e15

    with ExitStack() as ctx:
        def sb(name, shape, dt=F32):
            return ctx.enter_context(nc.sbuf_tensor("g_" + name, shape, dt))

        def ps(name, shape):
            return ctx.enter_context(nc.psum_tensor("g_" + name, shape, F32))

        def sem(name):
            return ctx.enter_context(nc.semaphore("g_" + name))

        rows = sb("rows", [P, N])
        e = sb("e", [P, N])
        mask = sb("mask", [P, N])
        s2_row = sb("s2_row", [P, N])
        x_sb = sb("x", [P, T, F])
        feat = sb("feat", [P, T, FE])
        x1 = sb("x1", [P, T, F])
        y = sb("y", [P, T, F])
        xT = mask[:]
        blk = sb("blk", [P, 2, SUPER])
        eye = sb("eye", [P, P])
        w0 = sb("w0", [P, FE])
        w0T = sb("w0T", [P, P])
        w1 = sb("w1", [P, P])
        w1T = sb("w1T", [P, P])
        wa2 = sb("wa2", [P, P])
        a_sb = sb("a", [P, 2])
        zeros = sb("zeros", [P, P])
        mhalf = sb("mhalf", [P, 1])
        dinv = sb("dinv", [P, T])
        h = sb("h", [P, F])
        he = sb("he", [P, F])
        hT = sb("hT", [P, F])
        o = sb("o", [P, F])
        negmax = sb("negmax", [P, 1])
        den = sb("den", [P, 1])
        rden = sb("rden", [P, 1])
        deg = sb("deg", [P, 1])
        deg_root = sb("deg_root", [P, 1])
        vpe = sb("vpe", [P, 1])
        rstd = sb("rstd", [P, 1])
        total = sb("total", [P, 1])
        sq = sb("sq", [P, 1])

        tb = ps("tb", [P, 2, SUPER])
        acc = ps("acc", [P, 2, SUPER])

        w_in = sem("w_in")
        x_in = sem("x_in")
        rows_in = sem("rows_in")
        const_set = sem("const_set")
        wT_ready = sem("wT_ready")
        wT_sb = sem("wT_sb")
        wa_ready = sem("wa_ready")
        wa_sb = sem("wa_sb")
        xT_ready = sem("xT_ready")
        xT_sb = sem("xT_sb")
        s2_ready = sem("s2_ready")
        s2_sb = sem("s2_sb")
        feat_ready = sem("feat_ready")
        feat_sb = sem("feat_sb")
        rows_used = sem("rows_used")
        masked = sem("masked")
        scores = sem("scores")
        probs = sem("probs")
        turned = sem("turned")
        copied = sem("copied")
        multiplied = sem("multiplied")
        dinv_root = sem("dinv_root")
        dinv_sb = sem("dinv_sb")
        rden_sb = sem("rden_sb")
        h_ready = sem("h_ready")
        neg_made = sem("neg_made")
        elu_exp = sem("elu_exp")
        elu_sum = sem("elu_sum")
        res_ready = sem("res_ready")
        mean_step = sem("mean_step")
        var_ready = sem("var_ready")
        rstd_ready = sem("rstd_ready")
        x1_ready = sem("x1_ready")
        y_ready = sem("y_ready")
        h_sb = sem("h_sb")
        h_turned = sem("h_turned")
        hT_sb = sem("hT_sb")
        z_ready = sem("z_ready")
        o_ready = sem("o_ready")
        out_st = sem("out_st")

        adj_v = adj.rearrange("(t p) c -> p t c", p=P)
        out_v = out.rearrange("(t p) f -> p t f", p=P)

        def one(v, t):
            return v[:, bass.ds(t, 1), :].rearrange("p o f -> p (o f)")

        block = ctx.enter_context(nc.Block())

        def where_needed(eng):
            needed = eng.value_load(flag[0:1, 0:1], min_val=0, max_val=1)
            return eng.If(needed != 0)

        @block.sync
        def _(sp):
            with where_needed(sp):
                sp.dma_start(eye[:], ident).then_inc(w_in, 16)
                sp.dma_start(w0[:, 0:F], w_gat).then_inc(w_in, 16)
                sp.dma_start(w1[:], w_gcn).then_inc(w_in, 16)
                with nc.allow_non_contiguous_dma(reason="the attention vector is tiny"):
                    sp.dma_start(a_sb[:], a_gat.rearrange("(k p) o -> p (k o)", p=P)).then_inc(w_in, 16)
                sp.dma_start(x_sb[:], x.rearrange("(t p) f -> p t f", p=P)).then_inc(x_in, 16)

                def load(t):
                    sp.dma_start(rows[:], one(adj_v, t)).then_inc(rows_in, 16)

                def store(t):
                    sp.wait_ge(o_ready, t + 1)
                    sp.dma_start(one(out_v, t), o[:]).then_inc(out_st, 16)

                load(0)
                with sp.Fori(1, T) as t:
                    sp.wait_ge(rows_used, t)
                    load(t)
                sp.wait_ge(rows_used, T)
                load(0)
                with sp.Fori(1, T) as t:
                    sp.wait_ge(turned, (T + t) * GROUPS)
                    load(t)
                    store(t - 1)
                store(T - 1)
                sp.wait_ge(out_st, 16 * T)

        @block.tensor
        def _(pe):
            with where_needed(pe):
                pe.wait_ge(w_in, 64)
                pe.transpose(tb[:, 0, 0:P], w0[:, 0:F], eye[:])
                pe.transpose(tb[:, 0, P:2 * P], w1[:], eye[:]).then_inc(wT_ready, 1)
                pe.wait_ge(wT_sb, 2)
                pe.matmul(acc[:, 0, 0:2], w0T[:], a_sb[:], start=True, stop=True).then_inc(wa_ready, 1)
                pe.wait_ge(x_in, 16)
                for g in range(GROUPS):
                    if g >= 1:
                        pe.wait_ge(xT_sb, g)
                    for a in range(G):
                        last = pe.transpose(tb[:, 0, a * P:(a + 1) * P], x_sb[:, g * G + a, :], eye[:])
                    last.then_inc(xT_ready, 1)
                pe.wait_ge(wa_sb, 2)
                pe.wait_ge(xT_sb, GROUPS)
                for g in range(GROUPS):
                    if g >= 1:
                        pe.wait_ge(s2_sb, g)
                    pe.matmul(tb[:, 0, :], wa2[:], xT[:, g * SUPER:(g + 1) * SUPER], start=True, stop=True
                              ).then_inc(s2_ready, 1)
                for t in range(T):
                    if t >= 1:
                        pe.wait_ge(feat_sb, t)
                    pe.matmul(acc[:, 0, 0:FE], xT[:, t * P:(t + 1) * P], w0[:], start=True, stop=True
                              ).then_inc(feat_ready, 1)
                pe.wait_ge(feat_sb, T)

                def aggregate(n, src, features):
                    def turn(g):
                        for a in range(G):
                            last = pe.transpose(tb[:, g % 2, a * P:(a + 1) * P],
                                                src[:, (g * G + a) * P:(g * G + a + 1) * P], eye[:])
                        last.then_inc(turned, 1)

                    turn(0)
                    for g in range(GROUPS):
                        if g + 1 < GROUPS:
                            turn(g + 1)
                        pe.wait_ge(copied, n * GROUPS + g + 1)
                        for a in range(G):
                            last = pe.matmul(acc[:, 0, 0:F], blk[:, g % 2, a * P:(a + 1) * P], features[:, g * G + a, 0:F],
                                             start=(g == 0 and a == 0), stop=(g == GROUPS - 1 and a == G - 1))
                        last.then_inc(multiplied, 1)

                with pe.Fori(0, T) as t:
                    pe.wait_ge(probs, t + 1)
                    aggregate(t, e[:], feat)

                def convolve(t):
                    pe.wait_ge(rows_in, (T + t) * 16 + 16)
                    aggregate(t + T, rows[:], y)
                    pe.wait_ge(h_sb, t + 1)
                    pe.transpose(tb[:, 0, 0:P], h[:], eye[:]).then_inc(h_turned, 1)
                    pe.wait_ge(hT_sb, t + 1)
                    pe.matmul(acc[:, 1, 0:F], hT[:], w1T[:], start=True, stop=True).then_inc(z_ready, 1)

                pe.wait_ge(y_ready, T)
                convolve(0)
                with pe.Fori(1, T) as t:
                    pe.wait_ge(o_ready, t)
                    convolve(t)

        @block.scalar
        def _(act):
            with where_needed(act):
                def copy_groups(n):
                    for g in range(GROUPS):
                        act.wait_ge(turned, n * GROUPS + g + 1)
                        if g >= 2:
                            act.wait_ge(multiplied, n * GROUPS + g - 1)
                        act.copy(blk[:, g % 2, :], tb[:, g % 2, :]).then_inc(copied, 1)

                with act.Fori(0, T) as t:
                    act.wait_ge(scores, t + 1)
                    act.activation(e[:], e[:], ACT.Exp, bias=negmax[:, 0:1], accum_out=den[:]).then_inc(probs, 1)
                    copy_groups(t)
                    act.wait_ge(neg_made, t + 1)
                    act.activation(he[:], he[:], ACT.Exp).then_inc(elu_exp, 1)

                def turn_sums(t):
                    copy_groups(t + T)
                    act.wait_ge(multiplied, (t + T) * GROUPS + GROUPS)
                    act.copy(h[:], acc[:, 0, 0:F]).then_inc(h_sb, 1)
                    act.wait_ge(h_turned, t + 1)
                    act.copy(hT[:], tb[:, 0, 0:P]).then_inc(hT_sb, 1)

                act.wait_ge(y_ready, T)
                turn_sums(0)
                with act.Fori(1, T) as t:
                    act.wait_ge(z_ready, t)
                    turn_sums(t)

        @block.gpsimd
        def _(pool):
            with where_needed(pool):
                pool.wait_ge(const_set, 2)
                with pool.Fori(0, T) as t:
                    pool.wait_ge(rows_used, t + 1)
                    pool.tensor_tensor(deg_root[:], deg[:], mhalf[:], ALU.pow).then_inc(dinv_root, 1)
                    pool.wait_ge(var_ready, t + 1)
                    pool.tensor_tensor(rstd[:], vpe[:], mhalf[:], ALU.pow).then_inc(rstd_ready, 1)
                with pool.Fori(T, 2 * T) as t:
                    pool.wait_ge(var_ready, t + 1)
                    pool.tensor_tensor(rstd[:], vpe[:], mhalf[:], ALU.pow).then_inc(rstd_ready, 1)

        @block.vector
        def _(dve):
            with where_needed(dve):
                dve.memset(mhalf[:], -0.5).then_inc(const_set, 1)
                dve.memset(zeros[:], 0.0).then_inc(const_set, 1)
                dve.wait_ge(wT_ready, 1)
                dve.tensor_copy(w0T[:], tb[:, 0, 0:P]).then_inc(wT_sb, 1)
                dve.tensor_copy(w1T[:], tb[:, 0, P:2 * P]).then_inc(wT_sb, 1)
                dve.wait_ge(wa_ready, 1)
                dve.wait_ge(const_set, 2)
                dve.tensor_copy(w0[:, F:FE], acc[:, 0, 0:2]).then_inc(wa_sb, 1)
                dve.tensor_scalar(wa2[:], zeros[:], acc[:, 0, 1:2], None, ALU.add).then_inc(wa_sb, 1)
                for g in range(GROUPS):
                    dve.wait_ge(xT_ready, g + 1)
                    dve.tensor_copy(xT[:, g * SUPER:(g + 1) * SUPER], tb[:, 0, :]).then_inc(xT_sb, 1)
                for g in range(GROUPS):
                    dve.wait_ge(s2_ready, g + 1)
                    dve.tensor_copy(s2_row[:, g * SUPER:(g + 1) * SUPER], tb[:, 0, :]).then_inc(s2_sb, 1)
                for t in range(T):
                    dve.wait_ge(feat_ready, t + 1)
                    dve.tensor_copy(feat[:, t, :], acc[:, 0, 0:FE]).then_inc(feat_sb, 1)
                dve.wait_ge(s2_sb, GROUPS)
                dve.wait_ge(feat_sb, T)

                def moments(n, v):
                    dve.wait_ge(res_ready, n + 1)
                    dve.tensor_reduce(total[:], v, AX_X, ALU.add).then_inc(mean_step, 1)
                    dve.wait_ge(mean_step, n * 4 + 1)
                    dve.tensor_scalar(total[:], total[:], 1.0 / F, None, ALU.mult).then_inc(mean_step, 1)
                    dve.wait_ge(mean_step, n * 4 + 2)
                    dve.tensor_scalar(v, v, total[:, 0:1], None, ALU.subtract).then_inc(mean_step, 1)
                    dve.wait_ge(mean_step, n * 4 + 3)
                    dve.scalar_tensor_tensor(he[:], v, 1.0, v, ALU.mult, ALU.mult, accum_out=sq[:]
                                             ).then_inc(mean_step, 1)
                    dve.wait_ge(mean_step, n * 4 + 4)
                    dve.tensor_scalar(vpe[:], sq[:], 1.0 / F, EPS, ALU.mult, ALU.add).then_inc(var_ready, 1)
                    dve.wait_ge(rstd_ready, n + 1)

                with dve.Fori(0, T) as t:
                    dve.wait_ge(rows_in, t * 16 + 16)
                    dve.tensor_scalar(mask[:], rows[:], 0.0, None, ALU.is_gt).then_inc(masked, 1)
                    s1 = feat[:, bass.ds(t, 1), F:F + 1].rearrange("p o f -> p (o f)")
                    dve.tensor_scalar(e[:], s2_row[:], s1, None, ALU.add).then_inc(masked, 1)
                    dve.wait_ge(masked, t * 6 + 2)
                    dve.scalar_tensor_tensor(e[:], e[:], SLOPE, e[:], ALU.mult, ALU.max).then_inc(masked, 1)
                    dve.wait_ge(masked, t * 6 + 3)
                    dve.tensor_tensor(e[:], e[:], mask[:], ALU.mult).then_inc(masked, 1)
                    dve.wait_ge(masked, t * 6 + 4)
                    dve.tensor_scalar(mask[:], mask[:], 1.0, NEG, ALU.subtract, ALU.mult).then_inc(masked, 1)
                    dve.wait_ge(masked, t * 6 + 5)
                    dve.tensor_tensor(e[:], e[:], mask[:], ALU.add).then_inc(masked, 1)
                    dve.wait_ge(masked, t * 6 + 6)
                    dve.tensor_reduce(negmax[:], e[:], AX_X, ALU.max, negate=True).then_inc(scores, 1)
                    dve.tensor_reduce(deg[:], rows[:], AX_X, ALU.add).then_inc(rows_used, 1)
                    dve.wait_ge(dinv_root, t + 1)
                    dve.tensor_copy(dinv[:, bass.ds(t, 1)], deg_root[:]).then_inc(dinv_sb, 1)
                    dve.wait_ge(probs, t + 1)
                    dve.reciprocal(rden[:], den[:]).then_inc(rden_sb, 1)
                    dve.wait_ge(rden_sb, t + 1)
                    dve.wait_ge(multiplied, t * GROUPS + GROUPS)
                    dve.tensor_scalar(h[:], acc[:, 0, 0:F], rden[:, 0:1], None, ALU.mult).then_inc(h_ready, 1)
                    dve.wait_ge(h_ready, t + 1)
                    dve.tensor_scalar(he[:], h[:], 0.0, None, ALU.min).then_inc(neg_made, 1)
                    dve.wait_ge(elu_exp, t + 1)
                    dve.scalar_tensor_tensor(h[:], h[:], 0.0, he[:], ALU.max, ALU.add).then_inc(elu_sum, 1)
                    dve.wait_ge(elu_sum, t + 1)
                    dve.scalar_tensor_tensor(h[:], h[:], -1.0, one(x_sb, t), ALU.add, ALU.add).then_inc(res_ready, 1)
                    moments(t, h[:])
                    dve.tensor_scalar(one(x1, t), h[:], rstd[:, 0:1], None, ALU.mult).then_inc(x1_ready, 1)
                    dve.wait_ge(x1_ready, t + 1)
                    dve.wait_ge(dinv_sb, t + 1)
                    dve.tensor_scalar(one(y, t), one(x1, t), dinv[:, bass.ds(t, 1)], None, ALU.mult
                                      ).then_inc(y_ready, 1)
                dve.wait_ge(y_ready, T)

                def layer1(t):
                    dve.wait_ge(z_ready, t + 1)
                    dve.scalar_tensor_tensor(o[:], acc[:, 1, 0:F], dinv[:, bass.ds(t, 1)], one(x1, t),
                                             ALU.mult, ALU.add).then_inc(res_ready, 1)
                    moments(t + T, o[:])
                    dve.tensor_scalar(o[:], o[:], rstd[:, 0:1], None, ALU.mult).then_inc(o_ready, 1)

                layer1(0)
                with dve.Fori(1, T) as t:
                    dve.wait_ge(out_st, t * 16)
                    layer1(t)


def build(nc, x, adj, w_gat, a_gat, w_gcn, ident, ident16, out):
    with ExitStack() as ctx:
        flag = ctx.enter_context(nc.sbuf_tensor("flag", [1, 1], I32))
        build_common(nc, x, adj, w_gat, a_gat, w_gcn, ident, ident16, out, flag)
        build_general(nc, x, adj, w_gat, a_gat, w_gcn, ident, out, flag)


_INS = ["x", "adj", "L0_gnn_W", "L0_gnn_a", "L1_gnn_W"]


def kernel(**inputs):
    import ml_dtypes
    import concourse.bacc as _bacc
    from concourse.bass_utils import run_bass_kernel_spmd as _run

    nc = _bacc.Bacc("TRN2", target_bir_lowering=False, num_devices=1)
    arrays, args = {}, []
    for name in _INS:
        a = np.ascontiguousarray(inputs[name])
        arrays[f"in_{name}"] = a
        args.append(nc.dram_tensor(f"in_{name}", a.shape, mybir.dt.from_np(a.dtype), kind="ExternalInput").ap())
    arrays["in_ident"] = np.eye(P, dtype=np.float32)
    arrays["in_ident16"] = np.eye(P, dtype=ml_dtypes.bfloat16)
    ident = nc.dram_tensor("in_ident", (P, P), F32, kind="ExternalInput").ap()
    ident16 = nc.dram_tensor("in_ident16", (P, P), BF16, kind="ExternalInput").ap()
    out = nc.dram_tensor("out_0", inputs["x"].shape, F32, kind="ExternalOutput").ap()
    build(nc, *args, ident, ident16, out)
    r = _run(nc, [arrays], core_ids=[0])
    return r.results[0]["out_0"]
```

```python
from contextlib import ExitStack

import numpy as np
import concourse.bass as bass
from concourse import mybir

ALU = mybir.AluOpType
ACT = mybir.ActivationFunctionType
F32 = mybir.dt.float32
BF16 = mybir.dt.bfloat16
FP8 = mybir.dt.float8e4
U8 = mybir.dt.uint8
I32 = mybir.dt.int32
AX_X = mybir.AxisListType.X

P = 128
SUPER = 512
TILES = SUPER // P
COLS = 1024
SLOTS = 2
QUAD = 4
BANKS = 4
RING = 4
AHEAD = 2
UNIT = 8
PARTS = 3
SCALED = 8
X_LOADS = 4
LATE_BUFS = 4
SLOPE = 0.2
EPS = 1e-5
SPREAD = 80.0


def build_common(nc, x, adj, w_gat, a_gat, w_gcn, ident, out, flag):
    N, F = x.shape
    U = N // SUPER
    JB = N // P
    CH = N // COLS
    QUADS = JB // QUAD
    QPC = QUADS // CH
    PIECES = CH * TILES
    PPQ = PIECES // QUADS
    LEAD = SLOTS * TILES // PPQ
    STEPS = U * JB
    FE = F + 2
    EARLY = PIECES // 2
    LATE = PIECES - EARLY
    assert LATE % LATE_BUFS == 0 and LATE // LATE_BUFS == TILES // 2
    assert QUADS % BANKS == 0 and JB % RING == 0 and SUPER == QUAD * P and PPQ == 2

    r_dram = nc.dram_tensor("r_scratch", (N,), F32, kind="Internal").ap()
    x1_dram = nc.dram_tensor("x1_scratch", (P, JB * F), F32, kind="Internal").ap()
    y_dram = nc.dram_tensor("y_scratch", (P, JB * PARTS * F), BF16, kind="Internal").ap()

    with ExitStack() as ctx:
        def sb(name, shape, dt=F32):
            return ctx.enter_context(nc.sbuf_tensor(name, shape, dt))

        def ps(name, shape):
            return ctx.enter_context(nc.psum_tensor(name, shape, F32))

        def sem(name):
            return ctx.enter_context(nc.semaphore(name))

        adjT = sb("adjT", [P, JB * N], FP8)
        chunk = sb("chunk", [P, SLOTS, TILES, COLS])
        feat = sb("feat", [P, JB, FE])
        blk = sb("blk", [P, RING, SUPER])
        r_row = sb("r_row", [P, 2, SUPER])
        h = sb("h", [P, TILES, F])
        he = sb("he", [P, TILES, F])
        x1 = sb("x1", [P, TILES, F])
        yp = sb("yp", [P, TILES, PARTS, F], BF16)
        adj8 = sb("adj8", [P, SLOTS, TILES, COLS], U8)
        marks = sb("marks", [P, COLS], U8)
        eye = sb("eye", [P, P])
        ones_col = sb("ones_col", [P, 1])
        q_col = sb("q_col", [P, JB])
        bad = sb("bad", [P, U * EARLY + 1])
        badc = sb("badc", [P, 2])
        dpart = sb("dpart", [P, 2, TILES, CH])
        dsum = sb("dsum", [P, TILES])
        dinv = sb("dinv", [P, JB])
        mhalf = sb("mhalf", [P, TILES])
        rden = sb("rden", [P, TILES])
        stats = sb("stats", [P, TILES, 6])
        mv = sb("mv", [P, TILES, 2])
        vpe = sb("vpe", [P, TILES])
        rstd = sb("rstd", [P, TILES])
        shift = sb("shift", [P, TILES])

        tb = ps("tb", [P, BANKS, SUPER])
        acc = ps("acc", [P, 4, SUPER])

        early = adjT[:].bitcast(F32)
        x_sb = early[:, 0:JB * F].rearrange("p (t f) -> p t f", f=F)
        xT = early[:, JB * F:2 * JB * F].rearrange("p (t f) -> p t f", f=F)
        w0 = early[:, 2 * JB * F:2 * JB * F + FE]
        w0T = early[:, 2 * JB * F + 256:2 * JB * F + 384]
        a_sb = early[:, 2 * JB * F + 512:2 * JB * F + 514]
        r_col = early[:, 2 * JB * F + 520:2 * JB * F + 520 + JB]
        rT = early[0:JB, 2 * JB * F + 640:2 * JB * F + 768]
        s_col = early[:, 2 * JB * F + 900:2 * JB * F + 900 + 2 * JB].rearrange("p (k t) -> p k t", k=2)
        g_col = early[:, 2 * JB * F + 970:2 * JB * F + 970 + JB]
        smax = early[:, 2 * JB * F + 1010:2 * JB * F + 1014]
        smax1 = early[0:2, 2 * JB * F + 1016:2 * JB * F + 1020]
        ones = early[0:2, 2 * JB * F + 768:2 * JB * F + 896]
        y_half = [chunk[:, s].rearrange("p a c -> p (a c)").bitcast(BF16)[:, 0:JB // 2 * PARTS * F]
                  .rearrange("p (t k f) -> p t k f", k=PARTS, f=F) for s in range(SLOTS)]
        x1_back = feat[:].rearrange("p t f -> p (t f)")[:, 0:2 * SUPER].rearrange("p (b a f) -> p b a f", b=2, f=F)
        late = [feat[:].rearrange("p t f -> p (t f)")[:, (2 + n) * SUPER:(2 + n) * SUPER + COLS] for n in (0, 2, 4)]
        late.append(chunk[:, 0].rearrange("p a c -> p (a c)")[:, (TILES - 1) * COLS:TILES * COLS])
        adjT_byte = adjT[:].rearrange("p (q i b) -> p q i b", i=N, b=QUAD)
        adjT_word = adjT[:].bitcast(I32).rearrange("p (q i) -> p q i", i=N)
        w1 = yp[:].rearrange("p a k f -> p (a k f)").bitcast(F32)[:, 0:P]
        w1T = yp[:].rearrange("p a k f -> p (a k f)").bitcast(F32)[:, P:2 * P]
        late_bad = adj8[:, 0, 1, :].bitcast(F32)
        adj8_word = adj8[:].rearrange("p s a c -> p (s a c)").bitcast(F32).rearrange(
            "p (s a w) -> p s a w", s=SLOTS, a=TILES)
        tb_word = tb[:].bitcast(I32)
        tb_byte = tb[:].bitcast(U8).rearrange("p k (i b) -> p k i b", b=QUAD)

        chunk_in = [sem(f"chunk_in{i}") for i in range(SLOTS)]
        r_in = [sem(f"r_in{i}") for i in range(2)]
        y_in = [sem(f"y_in{i}") for i in range(3)]
        x1_in = [sem(f"x1_in{i}") for i in range(2)]
        out_st = [sem(f"out_st{i}") for i in range(2)]
        late_in = [sem(f"late_in{i}") for i in range(LATE_BUFS)]
        x_in = [sem(f"x_in{i}") for i in range(X_LOADS)]
        xt_in = sem("xt_in")
        eye_in = sem("eye_in")
        w0_in = sem("w0_in")
        w1_in = sem("w1_in")
        const_set = sem("const_set")
        xT_ready = sem("xT_ready")
        xT_act = sem("xT_act")
        xT_dve = sem("xT_dve")
        w0T_ready = sem("w0T_ready")
        w0T_sb = sem("w0T_sb")
        w1T_ready = sem("w1T_ready")
        w1T_sb = sem("w1T_sb")
        wa_ready = sem("wa_ready")
        wa_sb = sem("wa_sb")
        feat_ready = sem("feat_ready")
        feat_act = sem("feat_act")
        feat_dve = sem("feat_dve")
        smax_col = sem("smax_col")
        smax_T = sem("smax_T")
        smax_one = sem("smax_one")
        smax_bc = sem("smax_bc")
        smax_sb = sem("smax_sb")
        s_prep = sem("s_prep")
        exps = sem("exps")
        rT_ready = sem("rT_ready")
        rT_sb = sem("rT_sb")
        r0_ready = sem("r0_ready")
        r0_sb = sem("r0_sb")
        r_stored = sem("r_stored")
        feat_scaled = sem("feat_scaled")

        t_ready = sem("t_ready")
        p_made = sem("p_made")
        kept = sem("kept")
        mm_done = sem("mm_done")
        summed = sem("summed")
        checked = sem("checked")
        late_checked = sem("late_checked")
        den_rec = sem("den_rec")
        acc_read = sem("acc_read")
        neg_made = sem("neg_made")
        elu_exp = sem("elu_exp")
        x_less = sem("x_less")
        exp_sum = sem("exp_sum")
        shift_ready = sem("shift_ready")
        res_ready = sem("res_ready")
        dsum_ready = sem("dsum_ready")
        dinv_ready = sem("dinv_ready")
        stat_ready = sem("stat_ready")
        mv_ready = sem("mv_ready")
        var_ready = sem("var_ready")
        rstd_ready = sem("rstd_ready")
        x1_ready = sem("x1_ready")
        y_ready = sem("y_ready")
        split = sem("split")
        x1_st = sem("x1_st")
        y_st = sem("y_st")
        conv_done = sem("conv_done")
        hT_sb = sem("hT_sb")
        z_ready = sem("z_ready")
        o_ready = sem("o_ready")
        bad_ready = sem("bad_ready")
        bad_sum = sem("bad_sum")
        flag_set = sem("flag_set")

        x_v = x.rearrange("(u p a) f -> u p a f", a=TILES, p=P)
        adj_v = adj.rearrange("(u p a) c -> u p a c", a=TILES, p=P)
        out_v = out.rearrange("(u p a) f -> u p a f", a=TILES, p=P)

        def at(v, u):
            return v[u] if isinstance(u, int) else v[bass.ds(u, 1)].rearrange("o p a f -> (o p) a f")

        def acc0(par):
            return acc[:, 2 * par:2 * par + 2, 0:2 * (F + 1)].rearrange("p b (a f) -> p b a f", a=2)

        half_tiles = [range(0, TILES // 2), range(TILES // 2, TILES)]
        half_rows = [slice(0, SUPER // 2), slice(SUPER // 2, SUPER)]

        def z_half(par, half):
            return tb[:, par if half != 1 else 1 - par, :]

        block = ctx.enter_context(nc.Block())

        @block.sync
        def _(sp):
            def load(u, c):
                sp.dma_start(chunk[:, c % SLOTS], at(adj_v, u)[:, :, c * COLS:(c + 1) * COLS]
                             ).then_inc(chunk_in[c % SLOTS], 16)

            def freed(u, c):
                n = (u * CH + c - SLOTS + 1) * TILES
                sp.wait_ge(summed, n)
                sp.wait_ge(checked, n)

            def load_r(u, par):
                sp.dma_start(r_row[:, par], r_dram[bass.ds(u * SUPER, SUPER)].partition_broadcast(P)
                             ).then_inc(r_in[par], 16)

            def load_xt(w):
                sp.dma_start(x1[:], at(x_v, w)).then_inc(xt_in, 16)

            sp.dma_start(eye[:], ident).then_inc(eye_in, 16)
            for q in range(X_LOADS):
                supers = slice(q * U // X_LOADS, (q + 1) * U // X_LOADS)
                sp.dma_start(x_sb[:, supers.start * TILES:supers.stop * TILES].rearrange("p (u a) f -> p u a f", a=TILES),
                             x_v[supers].rearrange("u p a f -> p u a f")).then_inc(x_in[q], 16)
                if q == 0:
                    sp.dma_start(w0[:, 0:F], w_gat).then_inc(w0_in, 16)
                    with nc.allow_non_contiguous_dma(reason="the attention vector is tiny"):
                        sp.dma_start(a_sb, a_gat.rearrange("(k p) o -> p (k o)", p=P)).then_inc(w0_in, 16)
            load(0, 0)
            load(0, 1)
            for c in range(SLOTS, CH):
                freed(0, c)
                load(0, c)
            sp.wait_ge(r_stored, 16)

            def super_loads(u, par, first=False):
                for c in range(CH):
                    freed(u, c)
                    load(u, c)
                    if c == 1:
                        if not first:
                            sp.wait_ge(p_made, (u - 1) * JB)
                        load_r(u, par)
                    if c == 3:
                        if not first:
                            sp.wait_ge(x1_st, (u - 1) * 16)
                        load_xt(u - 1)

            super_loads(1, 1, first=True)
            with sp.Fori(1, U // 2) as pair:
                super_loads(pair * 2, 0)
                super_loads(pair * 2 + 1, 1)
            half = JB // 2

            def load_y(n, s, lo, hi):
                freed(U, s)
                sp.wait_ge(y_st, 16 * ((s * half + hi) // TILES))
                cols = slice((s * half + lo) * PARTS * F, (s * half + hi) * PARTS * F)
                sp.dma_start(y_half[s][:, lo:hi].rearrange("p t k f -> p (t k f)"), y_dram[:, cols]
                             ).then_inc(y_in[n], 16)

            load_y(0, 0, 0, half)
            sp.wait_ge(x1_st, (U - 1) * 16)
            load_xt(U - 1)
            load_y(1, 1, 0, half - TILES)
            load_y(2, 1, half - TILES, half)

            def load_x1(w, par):
                sp.dma_start(x1_back[:, par].rearrange("p a f -> p (a f)"),
                             x1_dram[:, bass.ds(w * SUPER, SUPER)]).then_inc(x1_in[par], 16)

            def load_late(w, k):
                a, c = 2 * (k // CH) + 1, k % CH
                sp.dma_start(late[k % LATE_BUFS], at(adj_v, w)[:, a, c * COLS:(c + 1) * COLS]
                             ).then_inc(late_in[k % LATE_BUFS], 16)

            def load_late_rest(w, ks):
                for k in ks:
                    sp.wait_ge(late_checked, w * LATE + k - LATE_BUFS + 1)
                    load_late(w, k)

            sp.wait_ge(y_st, 16 * U)
            sp.dma_start(w1, w_gcn).then_inc(w1_in, 16)
            sp.wait_ge(mm_done, STEPS)
            sp.wait_ge(x1_st, 16 * U)
            load_x1(0, 0)
            load_x1(1, 1)
            for k in range(LATE_BUFS):
                load_late(0, k)
            load_late_rest(0, range(LATE_BUFS, LATE))
            load_late_rest(1, range(LATE))
            with sp.Fori(1, U // 2) as pair:
                for par in range(2):
                    w = pair * 2 + par
                    load_late_rest(w, range(LATE_BUFS))
                    sp.wait_ge(res_ready, U + w - 1)
                    load_x1(w, par)
                    load_late_rest(w, range(LATE_BUFS, LATE))

        @block.tensor
        def _(pe):
            def turn_x(q):
                pe.wait_ge(x_in[q], 16)
                for g in range(q * U // X_LOADS, (q + 1) * U // X_LOADS):
                    if g >= 2:
                        pe.wait_ge(xT_act if g % 2 == 0 else xT_dve, g // 2)
                    for a in range(TILES):
                        last = pe.transpose(tb[:, 2 + g % 2, a * P:(a + 1) * P], x_sb[:, g * TILES + a, :], eye[:])
                    last.then_inc(xT_ready, 1)

            def transposes(u, q):
                c, bank = q // QPC % CH, q % BANKS
                if q % QPC == 0:
                    pe.wait_ge(summed, (u * CH + q // QPC + 1) * TILES)
                for a in range(TILES):
                    col = q % QPC * P
                    last = pe.transpose(tb[:, bank, a * P:(a + 1) * P], adj8_word[:, c % SLOTS, a, col:col + P], eye[:])
                last.then_inc(t_ready, 1)

            def features(q):
                for t in range(q * JB // X_LOADS, (q + 1) * JB // X_LOADS):
                    g, b = t // TILES, (t // 2) % 4
                    if t % TILES == 0:
                        pe.wait_ge(xT_act if g % 2 == 0 else xT_dve, g // 2 + 1)
                    if t >= 8 and t % 2 == 0:
                        n = (t - 8) // 2
                        pe.wait_ge(feat_act if n % 2 == 0 else feat_dve, n // 2 + 1)
                    o = (t % 2) * FE
                    last = pe.matmul(acc[:, b, o:o + FE], xT[:, t, :], w0, start=(t % 2 == 0), stop=True,
                                     skip_group_check=True)
                    if t % 2:
                        last.then_inc(feat_ready, 1)

            pe.wait_ge(eye_in, 16)
            turn_x(0)
            pe.wait_ge(w0_in, 32)
            pe.transpose(tb[:, 0, 0:P], w0[:, 0:F], eye[:]).then_inc(w0T_ready, 1)
            turn_x(1)
            pe.wait_ge(w0T_sb, 1)
            pe.matmul(tb[:, 1, 0:2], w0T, a_sb, start=True, stop=True).then_inc(wa_ready, 1)
            pe.wait_ge(wa_sb, 1)
            features(0)
            for q in range(2, X_LOADS):
                turn_x(q)
                features(q - 1)
            features(X_LOADS - 1)
            pe.wait_ge(smax_col, 2)
            pe.transpose(tb[0:2, 0, 0:P], smax[:, 0:2], eye[:]).then_inc(smax_T, 1)
            pe.wait_ge(smax_one, 2)
            pe.matmul(tb[:, 1, 0:2], ones, smax1[:, 2:4], start=True, stop=True).then_inc(smax_bc, 1)
            pe.wait_ge(exps, 1)
            for a in range(TILES):
                last = pe.matmul(tb[:, 3, a * P:(a + 1) * P], r_col[:, a:a + 1].to_broadcast([P, P]), eye[:],
                                 start=(a == 0), stop=True, skip_group_check=True)
            last.then_inc(r0_ready, 1)
            pe.transpose(tb[0:JB, 2, 0:P], r_col, eye[:]).then_inc(rT_ready, 1)
            for q in range(AHEAD):
                transposes(0, q)
            pe.wait_ge(rT_sb, 1)
            pe.wait_ge(r0_sb, 1)

            def attend(u, par, last_super=False):
                sums = acc0(par)
                for q in range(QUADS):
                    late_turn = isinstance(u, int) and u == 0 and q == 0
                    if not late_turn and not (last_super and q + AHEAD >= QUADS):
                        if not (isinstance(u, int) and u == 0 and q + AHEAD < BANKS):
                            pe.wait_ge(kept, u * QUADS + q + AHEAD - BANKS + 1)
                        transposes(u, q + AHEAD)
                    for k in range(q * QUAD, (q + 1) * QUAD):
                        if isinstance(u, int) and u == 0 and k % SCALED == 0:
                            pe.wait_ge(feat_scaled, k // SCALED + 1)
                        pe.wait_ge(p_made, u * JB + k + 1)
                        for a in range(TILES):
                            last = pe.matmul(sums[:, a // 2, a % 2, :], blk[:, k % RING, a * P:(a + 1) * P],
                                             feat[:, k, 0:F + 1], start=(k == 0 and a % 2 == 0),
                                             stop=(k == JB - 1), skip_group_check=True)
                        last.then_inc(mm_done, 1)
                    if late_turn:
                        transposes(0, AHEAD)
                pe.wait_ge(acc_read, u)

            attend(0, 0)
            attend(1, 1)
            with pe.Fori(1, U // 2 - 1) as pair:
                attend(pair * 2, 0)
                attend(pair * 2 + 1, 1)
            attend(U - 2, 0)
            attend(U - 1, 1, last_super=True)

            def convolve(u, lo, hi, half=None):
                bank, rows = (u % 2, slice(0, SUPER)) if half is None else (2 + half, half_rows[half])
                if lo == 0:
                    pe.wait_ge(kept, (u + 1) * QUADS)
                    if u >= 2 and half is None:
                        pe.wait_ge(hT_sb, u - 1)
                for t in range(lo, hi):
                    if u == 0 and t in (0, JB // 2, JB - TILES):
                        pe.wait_ge(y_in[(0, JB // 2, JB - TILES).index(t)], 16)
                    for part in range(PARTS):
                        last = pe.matmul(acc[:, bank, rows], y_half[t // (JB // 2)][:, t % (JB // 2), part, :],
                                         adjT_byte[:, t // QUAD, u * SUPER + rows.start:u * SUPER + rows.stop, t % QUAD],
                                         start=(t == 0 and part == 0), stop=(t == JB - 1 and part == PARTS - 1))
                if hi == JB:
                    last.then_inc(conv_done, 1)

            def project(w, par, half=None):
                pe.wait_ge(hT_sb, w + 1 + (half or 0))
                if w >= 2:
                    pe.wait_ge(res_ready, U + w - 1 + (half or 0))
                tiles = range(TILES) if half is None else half_tiles[half]
                for a in tiles:
                    last = pe.matmul(z_half(par, half)[:, a * F:(a + 1) * F], blk[:, par, a * P:(a + 1) * P], w1T,
                                     start=(a == tiles[0]), stop=True, skip_group_check=True)
                last.then_inc(z_ready, 1)

            late_y = JB - TILES
            convolve(0, 0, late_y)
            convolve(1, 0, late_y)
            convolve(0, late_y, JB)
            convolve(1, late_y, JB)
            pe.wait_ge(kept, U * QUADS)
            pe.wait_ge(w1_in, 16)
            pe.transpose(tb[:, 3, 0:P], w1, eye[:]).then_inc(w1T_ready, 1)
            for u in range(2, U - 1):
                convolve(u, 0, JB // 4)
                if u == 2:
                    pe.wait_ge(w1T_sb, 1)
                if u == 2:
                    project(0, 0)
                project(u - 1, (u - 1) % 2)
                convolve(u, JB // 4, JB)
            convolve(U - 1, 0, JB // 2, half=0)
            project(U - 2, (U - 2) % 2)
            convolve(U - 1, JB // 2, JB, half=0)
            convolve(U - 1, 0, JB // 4, half=1)
            project(U - 1, (U - 1) % 2, half=0)
            convolve(U - 1, JB // 4, JB, half=1)
            pe.wait_ge(bad_ready, 2)
            pe.matmul(tb[0:1, 2, 0:1], badc[:, 0:1], ones_col[:], start=True, stop=False)
            pe.matmul(tb[0:1, 2, 0:1], badc[:, 1:2], ones_col[:], start=False, stop=True).then_inc(bad_sum, 1)
            project(U - 1, (U - 1) % 2, half=1)

        @block.scalar
        def _(act):
            def row_sum(n):
                g, a = n // TILES, n % TILES
                u, c = g // CH, g % CH
                if a == 0:
                    act.wait_ge(chunk_in[c % SLOTS], 16 * (g // SLOTS + 1))
                    if g >= SLOTS:
                        act.wait_ge(t_ready, (g - SLOTS + 1) * QPC)
                if u >= 2 and c == 0 and a == 0:
                    act.wait_ge(dsum_ready, u - 1)
                act.activation(adj8[:, c % SLOTS, a, :], chunk[:, c % SLOTS, a, :], ACT.Copy, scale=float(UNIT),
                               accum_out=dpart[:, u % 2, a, c:c + 1]).then_inc(summed, 1)

            def keep_features(q):
                for n in range(q * JB // X_LOADS // 2, (q + 1) * JB // X_LOADS // 2, 2):
                    act.wait_ge(feat_ready, n + 1)
                    act.copy(feat[:, 2 * n:2 * n + 2, :],
                             acc[:, n % 4, 0:2 * FE].rearrange("p (a n) -> p a n", a=2)).then_inc(feat_act, 1)

            for q in range(X_LOADS):
                g = 2 * q
                act.wait_ge(xT_ready, g + 1)
                act.copy(xT[:, g * TILES:(g + 1) * TILES, :],
                         tb[:, 2, :].rearrange("p (a n) -> p a n", a=TILES)).then_inc(xT_act, 1)
                if q >= 1:
                    keep_features(q - 1)
            row_sum(0)
            row_sum(1)
            keep_features(X_LOADS - 1)
            row_sum(2)
            row_sum(3)
            act.wait_ge(s_prep, 2)
            act.activation(r_col, s_col[:, 0, :], ACT.Exp, scale=-(1.0 - SLOPE)).then_inc(exps, 1)
            act.activation(q_col[:], s_col[:, 1, :], ACT.Exp, scale=1.0 - SLOPE).then_inc(exps, 1)
            act.activation(g_col, s_col[:, 1, :], ACT.Exp, scale=SLOPE).then_inc(exps, 1)
            act.wait_ge(r0_ready, 1)
            act.copy(r_row[:, 0, :], tb[:, 3, :]).then_inc(r0_sb, 1)
            act.wait_ge(rT_ready, 1)
            act.copy(rT, tb[0:JB, 2, 0:P]).then_inc(rT_sb, 1)
            act.wait_ge(rT_sb, 1)
            act.dma_start(r_dram.rearrange("(t p) -> t p", p=P), rT).then_inc(r_stored, 16)

            def keep(u, q):
                act.wait_ge(p_made, u * JB + (q + 1) * QUAD)
                act.copy(adjT_word[:, q, u * SUPER:(u + 1) * SUPER], tb_word[:, q % BANKS, :]).then_inc(kept, 1)

            def weigh(w):
                par = w % 2
                act.wait_ge(den_rec, w + 1)
                if w >= 1:
                    act.wait_ge(x1_ready, w)
                    act.wait_ge(split, 5 * w)
                for a in range(TILES):
                    last = act.activation(h[:, a, :], acc0(par)[:, a // 2, a % 2, 0:F], ACT.Copy,
                                          scale=rden[:, a:a + 1])
                last.then_inc(acc_read, 1)
                act.wait_ge(acc_read, w + 1)
                act.activation(he[:], h[:], ACT.Relu, scale=-1.0).then_inc(neg_made, 1)
                act.wait_ge(neg_made, w + 1)
                act.activation(he[:], he[:], ACT.Exp, scale=-1.0).then_inc(elu_exp, 1)

            def layer0_out(w):
                act.wait_ge(shift_ready, w + 1)
                for a in range(TILES):
                    last = act.activation(x1[:, a, :], h[:, a, :], ACT.Identity, bias=shift[:, a:a + 1],
                                          scale=rstd[:, a:a + 1])
                last.then_inc(x1_ready, 1)

            def scale_y(w):
                act.wait_ge(x1_ready, w + 1)
                act.wait_ge(dinv_ready, w + 1)
                for a in range(TILES):
                    t = w * TILES + a
                    last = act.activation(he[:, a, :], x1[:, a, :], ACT.Copy, scale=dinv[:, t:t + 1])
                last.then_inc(y_ready, 1)

            for n in range(TILES, LEAD * PPQ):
                row_sum(n)
            act.wait_ge(r_stored, 16)
            for u in range(U):
                for q in range(QUADS):
                    if q % QPC == 0 and (u * QUADS + q + LEAD) * PPQ < U * PIECES:
                        for a in range(TILES):
                            row_sum((u * QUADS + q + LEAD) * PPQ + a)
                    keep(u, q)
                    if u >= 1 and q == 1:
                        weigh(u - 1)
                    if u >= 1 and q == 5:
                        layer0_out(u - 1)
                        scale_y(u - 1)
            weigh(U - 1)
            layer0_out(U - 1)
            scale_y(U - 1)

            def copy_hT(w, par, half=None):
                act.wait_ge(conv_done, w + 1 + (half or 0))
                bank, rows = (par, slice(0, SUPER)) if half is None else (2 + half, half_rows[half])
                act.activation(blk[:, par, rows], acc[:, bank, rows], ACT.Copy, scale=64.0 * UNIT).then_inc(hT_sb, 1)

            def store(w, par, half=None):
                act.wait_ge(o_ready, w + 1 + (half or 0))
                dst, rows = (at(out_v, w), slice(0, SUPER)) if half is None else (
                    at(out_v, w)[:, half_tiles[half].start:half_tiles[half].stop], half_rows[half])
                act.dma_start(dst, blk[:, 2 + par, rows].rearrange("p (a f) -> p a f", f=F)
                              ).then_inc(out_st[par], 16)

            copy_hT(0, 0)
            copy_hT(1, 1)
            act.wait_ge(w1T_ready, 1)
            act.copy(w1T, tb[:, 3, 0:P]).then_inc(w1T_sb, 1)
            def layer1_step(w, par):
                act.wait_ge(z_ready, w - 1)
                copy_hT(w, par)
                store(w - 2, par)

            with act.Fori(1, U // 2 - 1) as pair:
                for par in range(2):
                    layer1_step(pair * 2 + par, par)
            layer1_step(U - 2, 0)
            act.wait_ge(z_ready, U - 2)
            copy_hT(U - 1, 1, half=0)
            store(U - 3, 1)
            store(U - 2, 0)
            copy_hT(U - 1, 1, half=1)
            store(U - 1, 1, half=0)
            store(U - 1, 1, half=1)
            act.wait_ge(out_st[0], 16 * (U // 2))
            act.wait_ge(out_st[1], 16 * (U // 2 + 1))

        @block.gpsimd
        def _(pool):
            def root(n, dst, src, ready, done):
                pool.wait_ge(ready, n + 1)
                pool.tensor_tensor(dst, src, mhalf[:], ALU.pow).then_inc(done, 1)

            def elu_less(w):
                pool.wait_ge(xt_in, w * 16 + 16)
                pool.tensor_scalar(x1[:], x1[:], 1.0, -1.0, ALU.mult, ALU.add).then_inc(x_less, 1)
                pool.wait_ge(x_less, w + 1)
                pool.wait_ge(elu_exp, w + 1)
                pool.tensor_tensor(he[:], he[:], x1[:], ALU.add).then_inc(exp_sum, 1)

            def parts(w):
                pool.wait_ge(y_ready, w + 1)
                pool.dma_start(x1_dram[:, w * SUPER:(w + 1) * SUPER],
                               x1[:].rearrange("p a f -> p (a f)")).then_inc(x1_st, 16)
                pool.wait_ge(y_st, 16 * w)
                for part in range(PARTS):
                    pool.tensor_copy(yp[:, :, part, :], he[:]).then_inc(split, 1)
                    pool.wait_ge(split, w * 5 + 2 * part + 1)
                    if part < PARTS - 1:
                        pool.tensor_tensor(he[:], he[:], yp[:, :, part, :], ALU.subtract).then_inc(split, 1)
                        pool.wait_ge(split, w * 5 + 2 * part + 2)
                pool.dma_start(y_dram[:, w * SUPER * PARTS:(w + 1) * SUPER * PARTS],
                               yp[:].rearrange("p a k f -> p (a k f)")).then_inc(y_st, 16)

            pool.wait_ge(const_set, 4)
            for w in range(U):
                root(w, dinv[:, w * TILES:(w + 1) * TILES], dsum[:], dsum_ready, dinv_ready)
                elu_less(w)
                root(w, rstd[:], vpe[:], var_ready, rstd_ready)
                parts(w)
            for w in range(U - 1):
                root(U + w, rstd[:], vpe[:], var_ready, rstd_ready)
            for half, tiles in enumerate(half_tiles):
                cols = slice(tiles.start, tiles.stop)
                pool.wait_ge(var_ready, 2 * U + half)
                pool.tensor_tensor(rstd[:, cols], vpe[:, cols], mhalf[:, cols], ALU.pow).then_inc(rstd_ready, 1)
            pool.wait_ge(y_st, 16 * U)
            pool.wait_ge(x1_st, 16 * U)

        @block.vector
        def _(dve):
            dve.memset(ones, 1.0).then_inc(const_set, 1)
            dve.memset(mhalf[:], -0.5).then_inc(const_set, 1)
            dve.memset(ones_col[:], 1.0).then_inc(const_set, 1)
            dve.memset(bad[:], 0.0).then_inc(const_set, 1)

            def count_bad(piece, marks, counts, n):
                return dve.scalar_tensor_tensor(marks, piece, 1.0, piece, ALU.not_equal,
                                                ALU.logical_and, accum_out=counts[:, bass.ds(n, 1)])

            def check(u, k):
                n = u * EARLY + k
                c, a = k // 2 % CH, k % 2 * 2
                if a == 0:
                    dve.wait_ge(chunk_in[c % SLOTS], 16 * (u * (CH // SLOTS) + k // 2 // SLOTS + 1))
                if not (isinstance(n, int) and n < 1):
                    dve.wait_ge(checked, n * 2)
                count_bad(chunk[:, c % SLOTS, a, :], marks[:], bad, n).then_inc(checked, 2)

            def keep_features(q):
                for n in range(q * JB // X_LOADS // 2 + 1, (q + 1) * JB // X_LOADS // 2, 2):
                    dve.wait_ge(feat_ready, n + 1)
                    dve.tensor_copy(feat[:, 2 * n:2 * n + 2, :],
                                    acc[:, n % 4, 0:2 * FE].rearrange("p (a n) -> p a n", a=2)).then_inc(feat_dve, 1)

            for q in range(X_LOADS):
                g = 2 * q + 1
                dve.wait_ge(xT_ready, g + 1)
                dve.tensor_copy(xT[:, g * TILES:(g + 1) * TILES, :],
                                tb[:, 3, :].rearrange("p (a n) -> p a n", a=TILES)).then_inc(xT_dve, 1)
                if q == 0:
                    dve.wait_ge(w0T_ready, 1)
                    dve.tensor_copy(w0T, tb[:, 0, 0:P]).then_inc(w0T_sb, 1)
                if q == 1:
                    dve.wait_ge(wa_ready, 1)
                    dve.tensor_copy(w0[:, F:FE], tb[:, 1, 0:2]).then_inc(wa_sb, 1)
                if q >= 1:
                    keep_features(q - 1)
            dve.wait_ge(const_set, 4)
            check(0, 0)
            check(0, 1)
            keep_features(X_LOADS - 1)
            dve.wait_ge(feat_act, JB // 4)
            dve.wait_ge(feat_dve, JB // 4)
            dve.tensor_reduce(smax[:, 0:1], feat[:, :, F + 1], AX_X, ALU.max).then_inc(smax_col, 1)
            dve.tensor_reduce(smax[:, 1:2], feat[:, :, F + 1], AX_X, ALU.min, negate=True).then_inc(smax_col, 1)
            dve.wait_ge(smax_T, 1)
            dve.tensor_reduce(smax1[:, 0:1], tb[0:2, 0, 0:P], AX_X, ALU.max).then_inc(smax_one, 1)
            dve.wait_ge(smax_one, 1)
            dve.wait_ge(eye_in, 16)
            dve.tensor_scalar(smax1[:, 2:4], eye[0:2, 0:2], smax1[:, 0:1], None, ALU.mult).then_inc(smax_one, 1)
            dve.wait_ge(smax_bc, 1)
            dve.tensor_copy(smax[:, 2:4], tb[:, 1, 0:2]).then_inc(smax_sb, 1)
            dve.wait_ge(smax_sb, 1)
            dve.tensor_scalar(s_col[:, 0, :], feat[:, :, F], smax[:, 2:3], 0.0, ALU.add, ALU.max).then_inc(s_prep, 1)
            dve.tensor_scalar(s_col[:, 1, :], feat[:, :, F + 1], smax[:, 2:3], -SPREAD, ALU.subtract, ALU.max
                              ).then_inc(s_prep, 1)
            dve.wait_ge(const_set, 4)
            dve.tensor_scalar(bad[:, U * EARLY:], smax[:, 2:3], smax[:, 3:4], SPREAD, ALU.add, ALU.is_gt
                              ).then_inc(s_prep, 1)
            dve.wait_ge(s_prep, 3)
            dve.memset(feat[:, :, F:F + 1], 1.0).then_inc(s_prep, 1)
            dve.wait_ge(s_prep, 4)
            def late_checks(w):
                for k in range(LATE):
                    n = w * LATE + k
                    if k % LATE_BUFS == k:
                        dve.wait_ge(late_in[k % LATE_BUFS], w * 32 + 16)
                    else:
                        dve.wait_ge(late_in[k % LATE_BUFS], w * 32 + 32)
                    if not (isinstance(n, int) and n < 2):
                        dve.wait_ge(late_checked, n - 1)
                    count_bad(late[k % LATE_BUFS], adj8[:, k % 2, 0, :], late_bad, n).then_inc(late_checked, 1)

            dve.wait_ge(exps, 3)

            def scale(part):
                tiles = slice(part * SCALED, (part + 1) * SCALED)
                dve.tensor_tensor(feat[:, tiles, 0:F + 1], feat[:, tiles, 0:F + 1],
                                  g_col[:, tiles].rearrange("p (t o) -> p t o", o=1).to_broadcast([P, SCALED, F + 1]),
                                  ALU.mult).then_inc(feat_scaled, 1)

            def weights(u, k, par):
                if k == 0:
                    if isinstance(u, int) and u == 0:
                        dve.wait_ge(r0_sb, 1)
                    else:
                        dve.wait_ge(r_in[par], (u - par) * 8 + 16 * par)
                if k % QUAD == 0:
                    dve.wait_ge(t_ready, u * QUADS + k // QUAD + 1)
                if not (isinstance(u, int) and u == 0 and k < RING):
                    dve.wait_ge(mm_done, u * JB + k + 1 - RING)
                dve.scalar_tensor_tensor(blk[:, k % RING, :], r_row[:, par, :], q_col[:, k:k + 1],
                                         tb_byte[:, k // QUAD % BANKS, :, k % QUAD], ALU.max, ALU.mult
                                         ).then_inc(p_made, 1)

            def attend(u, par, prev=True, last_super=False):
                for q in range(QUADS):
                    for b in range(QUAD):
                        weights(u, q * QUAD + b, par)
                        if not prev and q < QPC:
                            if b % 2 == 0:
                                check(u, 2 + 2 * q + b // 2)
                        elif q % QPC == 0 and b % 2 == 0 and not (last_super and q + LEAD >= QUADS):
                            check(u, q + LEAD + b // 2)
                    if not prev and q % 2 == 0 and q // 2 + 1 < JB // SCALED:
                        scale(q // 2 + 1)
                    if prev:
                        w, wp = u - 1, 1 - par
                        if q == 0:
                            denominators(w, wp)
                        if q == 1:
                            degrees(w, wp)
                        if q == 3:
                            residual(w)
                            moments(w)
                        if q == 5:
                            layer0_shift(w)

            def denominators(w, par):
                dve.wait_ge(mm_done, (w + 1) * JB)
                dve.wait_ge(acc_read, w)
                dve.reciprocal(rden[:].rearrange("p (b a) -> p b a", a=2), acc0(par)[:, :, :, F]).then_inc(den_rec, 1)

            def degrees(w, par):
                dve.wait_ge(summed, (w + 1) * PIECES)
                dve.wait_ge(dinv_ready, w)
                dve.tensor_reduce(dsum[:], dpart[:, par], AX_X, ALU.add).then_inc(dsum_ready, 1)

            def residual(w):
                dve.wait_ge(exp_sum, w + 1)
                dve.scalar_tensor_tensor(h[:], h[:], 0.0, he[:], ALU.max, ALU.add).then_inc(res_ready, 1)

            def moments(n, tiles=range(TILES)):
                dve.wait_ge(res_ready, n + 1)
                for a in tiles:
                    last = dve.bn_stats(stats[:, a, :], h[:, a, :])
                last.then_inc(stat_ready, 1)
                dve.wait_ge(const_set, 4)
                dve.wait_ge(stat_ready, n + 1)
                for a in tiles:
                    last = dve.bn_aggr(mv[:, a, :], stats[:, a, :])
                last.then_inc(mv_ready, 1)
                dve.wait_ge(mv_ready, n + 1)
                cols = slice(tiles.start, tiles.stop)
                dve.tensor_scalar(vpe[:, cols], mv[:, cols, 1], EPS, None, ALU.add).then_inc(var_ready, 1)

            def layer0_shift(w):
                dve.wait_ge(rstd_ready, w + 1)
                dve.scalar_tensor_tensor(shift[:], mv[:, :, 0], -1.0, rstd[:], ALU.mult, ALU.mult
                                         ).then_inc(shift_ready, 1)

            scale(0)
            attend(0, 0, prev=False)
            attend(1, 1)
            with dve.Fori(1, U // 2 - 1) as pair:
                attend(pair * 2, 0)
                attend(pair * 2 + 1, 1)
            attend(U - 2, 0)
            attend(U - 1, 1, last_super=True)
            w = U - 1
            denominators(w, 1)
            degrees(w, 1)
            residual(w)
            moments(w)
            layer0_shift(w)
            dve.wait_ge(t_ready, U * QUADS)

            def layer1_res(w, par, half=None):
                if isinstance(w, int) and w == 0:
                    dve.wait_ge(x1_ready, U)
                elif half != 1:
                    dve.wait_ge(o_ready, w)
                dve.wait_ge(z_ready, w + 1 + (half or 0))
                dve.wait_ge(x1_in[par], (w - par) * 8 + 16)
                for a in range(TILES) if half is None else half_tiles[half]:
                    last = dve.scalar_tensor_tensor(
                        h[:, a, :], z_half(par, half)[:, a * F:(a + 1) * F], dinv[:, bass.ds(w * TILES + a, 1)],
                        x1_back[:, par, a, :], ALU.mult, ALU.add)
                last.then_inc(res_ready, 1)

            def layer1_out(w, par, stored, half=None):
                if stored is not None:
                    dve.wait_ge(out_st[par], stored)
                dve.wait_ge(rstd_ready, U + w + 1 + (half or 0))
                for a in range(TILES) if half is None else half_tiles[half]:
                    last = dve.tensor_scalar(blk[:, 2 + par, a * F:(a + 1) * F], h[:, a, :], mv[:, a, 0:1],
                                             rstd[:, a:a + 1], ALU.subtract, ALU.mult)
                last.then_inc(o_ready, 1)

            late_checks(0)
            for w in range(2):
                late_checks(w + 1)
                layer1_res(w, w)
                moments(U + w)
                layer1_out(w, w, None)
            with dve.Fori(1, U // 2 - 1) as pair:
                for par in range(2):
                    w = pair * 2 + par
                    late_checks(w + 1)
                    layer1_res(w, par)
                    moments(w + U)
                    layer1_out(w, par, (w - par) * 8)
            late_checks(U - 1)
            dve.wait_ge(late_checked, U * LATE)
            dve.tensor_reduce(badc[:, 0:1], bad[:], AX_X, ALU.add).then_inc(bad_ready, 1)
            dve.tensor_reduce(badc[:, 1:2], late_bad[:, 0:U * LATE], AX_X, ALU.add).then_inc(bad_ready, 1)
            layer1_res(U - 2, 0)
            moments(U - 2 + U)
            layer1_out(U - 2, 0, (U - 2) * 8)
            for half in range(2):
                layer1_res(U - 1, 1, half)
                moments(U - 1 + U + half, half_tiles[half])
                layer1_out(U - 1, 1, (U - 2) * 8, half)
            dve.wait_ge(bad_sum, 1)
            dve.tensor_scalar(flag[:], tb[0:1, 2, 0:1], 0.0, None, ALU.is_gt).then_inc(flag_set, 1)


def build_general(nc, x, adj, w_gat, a_gat, w_gcn, ident, out, flag):
    N, F = x.shape
    T = N // P
    G = SUPER // P
    GROUPS = T // G
    FE = F + 2
    NEG = 9e15

    with ExitStack() as ctx:
        def sb(name, shape, dt=F32):
            return ctx.enter_context(nc.sbuf_tensor("g_" + name, shape, dt))

        def ps(name, shape):
            return ctx.enter_context(nc.psum_tensor("g_" + name, shape, F32))

        def sem(name):
            return ctx.enter_context(nc.semaphore("g_" + name))

        rows = sb("rows", [P, N])
        e = sb("e", [P, N])
        mask = sb("mask", [P, N])
        s2_row = sb("s2_row", [P, N])
        x_sb = sb("x", [P, T, F])
        feat = sb("feat", [P, T, FE])
        x1 = sb("x1", [P, T, F])
        y = sb("y", [P, T, F])
        xT = mask[:]
        blk = sb("blk", [P, 2, SUPER])
        eye = sb("eye", [P, P])
        w0 = sb("w0", [P, FE])
        w0T = sb("w0T", [P, P])
        w1 = sb("w1", [P, P])
        w1T = sb("w1T", [P, P])
        wa2 = sb("wa2", [P, P])
        a_sb = sb("a", [P, 2])
        zeros = sb("zeros", [P, P])
        mhalf = sb("mhalf", [P, 1])
        dinv = sb("dinv", [P, T])
        h = sb("h", [P, F])
        he = sb("he", [P, F])
        hT = sb("hT", [P, F])
        o = sb("o", [P, F])
        negmax = sb("negmax", [P, 1])
        den = sb("den", [P, 1])
        rden = sb("rden", [P, 1])
        deg = sb("deg", [P, 1])
        deg_root = sb("deg_root", [P, 1])
        vpe = sb("vpe", [P, 1])
        rstd = sb("rstd", [P, 1])
        total = sb("total", [P, 1])
        sq = sb("sq", [P, 1])

        tb = ps("tb", [P, 2, SUPER])
        acc = ps("acc", [P, 2, SUPER])

        w_in = sem("w_in")
        x_in = sem("x_in")
        rows_in = sem("rows_in")
        const_set = sem("const_set")
        wT_ready = sem("wT_ready")
        wT_sb = sem("wT_sb")
        wa_ready = sem("wa_ready")
        wa_sb = sem("wa_sb")
        xT_ready = sem("xT_ready")
        xT_sb = sem("xT_sb")
        s2_ready = sem("s2_ready")
        s2_sb = sem("s2_sb")
        feat_ready = sem("feat_ready")
        feat_sb = sem("feat_sb")
        rows_used = sem("rows_used")
        masked = sem("masked")
        scores = sem("scores")
        probs = sem("probs")
        turned = sem("turned")
        copied = sem("copied")
        multiplied = sem("multiplied")
        dinv_root = sem("dinv_root")
        dinv_sb = sem("dinv_sb")
        rden_sb = sem("rden_sb")
        h_ready = sem("h_ready")
        neg_made = sem("neg_made")
        elu_exp = sem("elu_exp")
        elu_sum = sem("elu_sum")
        res_ready = sem("res_ready")
        mean_step = sem("mean_step")
        var_ready = sem("var_ready")
        rstd_ready = sem("rstd_ready")
        x1_ready = sem("x1_ready")
        y_ready = sem("y_ready")
        h_sb = sem("h_sb")
        h_turned = sem("h_turned")
        hT_sb = sem("hT_sb")
        z_ready = sem("z_ready")
        o_ready = sem("o_ready")
        out_st = sem("out_st")

        adj_v = adj.rearrange("(t p) c -> p t c", p=P)
        out_v = out.rearrange("(t p) f -> p t f", p=P)

        def one(v, t):
            return v[:, bass.ds(t, 1), :].rearrange("p o f -> p (o f)")

        block = ctx.enter_context(nc.Block())

        def where_needed(eng):
            needed = eng.value_load(flag[0:1, 0:1], min_val=0, max_val=1)
            return eng.If(needed != 0)

        @block.sync
        def _(sp):
            with where_needed(sp):
                sp.dma_start(eye[:], ident).then_inc(w_in, 16)
                sp.dma_start(w0[:, 0:F], w_gat).then_inc(w_in, 16)
                sp.dma_start(w1[:], w_gcn).then_inc(w_in, 16)
                with nc.allow_non_contiguous_dma(reason="the attention vector is tiny"):
                    sp.dma_start(a_sb[:], a_gat.rearrange("(k p) o -> p (k o)", p=P)).then_inc(w_in, 16)
                sp.dma_start(x_sb[:], x.rearrange("(t p) f -> p t f", p=P)).then_inc(x_in, 16)

                def load(t):
                    sp.dma_start(rows[:], one(adj_v, t)).then_inc(rows_in, 16)

                def store(t):
                    sp.wait_ge(o_ready, t + 1)
                    sp.dma_start(one(out_v, t), o[:]).then_inc(out_st, 16)

                load(0)
                with sp.Fori(1, T) as t:
                    sp.wait_ge(rows_used, t)
                    load(t)
                sp.wait_ge(rows_used, T)
                load(0)
                with sp.Fori(1, T) as t:
                    sp.wait_ge(turned, (T + t) * GROUPS)
                    load(t)
                    store(t - 1)
                store(T - 1)
                sp.wait_ge(out_st, 16 * T)

        @block.tensor
        def _(pe):
            with where_needed(pe):
                pe.wait_ge(w_in, 64)
                pe.transpose(tb[:, 0, 0:P], w0[:, 0:F], eye[:])
                pe.transpose(tb[:, 0, P:2 * P], w1[:], eye[:]).then_inc(wT_ready, 1)
                pe.wait_ge(wT_sb, 2)
                pe.matmul(acc[:, 0, 0:2], w0T[:], a_sb[:], start=True, stop=True).then_inc(wa_ready, 1)
                pe.wait_ge(x_in, 16)
                for g in range(GROUPS):
                    if g >= 1:
                        pe.wait_ge(xT_sb, g)
                    for a in range(G):
                        last = pe.transpose(tb[:, 0, a * P:(a + 1) * P], x_sb[:, g * G + a, :], eye[:])
                    last.then_inc(xT_ready, 1)
                pe.wait_ge(wa_sb, 2)
                pe.wait_ge(xT_sb, GROUPS)
                for g in range(GROUPS):
                    if g >= 1:
                        pe.wait_ge(s2_sb, g)
                    pe.matmul(tb[:, 0, :], wa2[:], xT[:, g * SUPER:(g + 1) * SUPER], start=True, stop=True
                              ).then_inc(s2_ready, 1)
                for t in range(T):
                    if t >= 1:
                        pe.wait_ge(feat_sb, t)
                    pe.matmul(acc[:, 0, 0:FE], xT[:, t * P:(t + 1) * P], w0[:], start=True, stop=True
                              ).then_inc(feat_ready, 1)
                pe.wait_ge(feat_sb, T)

                def aggregate(n, src, features):
                    def turn(g):
                        for a in range(G):
                            last = pe.transpose(tb[:, g % 2, a * P:(a + 1) * P],
                                                src[:, (g * G + a) * P:(g * G + a + 1) * P], eye[:])
                        last.then_inc(turned, 1)

                    turn(0)
                    for g in range(GROUPS):
                        if g + 1 < GROUPS:
                            turn(g + 1)
                        pe.wait_ge(copied, n * GROUPS + g + 1)
                        for a in range(G):
                            last = pe.matmul(acc[:, 0, 0:F], blk[:, g % 2, a * P:(a + 1) * P], features[:, g * G + a, 0:F],
                                             start=(g == 0 and a == 0), stop=(g == GROUPS - 1 and a == G - 1))
                        last.then_inc(multiplied, 1)

                with pe.Fori(0, T) as t:
                    pe.wait_ge(probs, t + 1)
                    aggregate(t, e[:], feat)

                def convolve(t):
                    pe.wait_ge(rows_in, (T + t) * 16 + 16)
                    aggregate(t + T, rows[:], y)
                    pe.wait_ge(h_sb, t + 1)
                    pe.transpose(tb[:, 0, 0:P], h[:], eye[:]).then_inc(h_turned, 1)
                    pe.wait_ge(hT_sb, t + 1)
                    pe.matmul(acc[:, 1, 0:F], hT[:], w1T[:], start=True, stop=True).then_inc(z_ready, 1)

                pe.wait_ge(y_ready, T)
                convolve(0)
                with pe.Fori(1, T) as t:
                    pe.wait_ge(o_ready, t)
                    convolve(t)

        @block.scalar
        def _(act):
            with where_needed(act):
                def copy_groups(n):
                    for g in range(GROUPS):
                        act.wait_ge(turned, n * GROUPS + g + 1)
                        if g >= 2:
                            act.wait_ge(multiplied, n * GROUPS + g - 1)
                        act.copy(blk[:, g % 2, :], tb[:, g % 2, :]).then_inc(copied, 1)

                with act.Fori(0, T) as t:
                    act.wait_ge(scores, t + 1)
                    act.activation(e[:], e[:], ACT.Exp, bias=negmax[:, 0:1], accum_out=den[:]).then_inc(probs, 1)
                    copy_groups(t)
                    act.wait_ge(neg_made, t + 1)
                    act.activation(he[:], he[:], ACT.Exp).then_inc(elu_exp, 1)

                def turn_sums(t):
                    copy_groups(t + T)
                    act.wait_ge(multiplied, (t + T) * GROUPS + GROUPS)
                    act.copy(h[:], acc[:, 0, 0:F]).then_inc(h_sb, 1)
                    act.wait_ge(h_turned, t + 1)
                    act.copy(hT[:], tb[:, 0, 0:P]).then_inc(hT_sb, 1)

                act.wait_ge(y_ready, T)
                turn_sums(0)
                with act.Fori(1, T) as t:
                    act.wait_ge(z_ready, t)
                    turn_sums(t)

        @block.gpsimd
        def _(pool):
            with where_needed(pool):
                pool.wait_ge(const_set, 2)
                with pool.Fori(0, T) as t:
                    pool.wait_ge(rows_used, t + 1)
                    pool.tensor_tensor(deg_root[:], deg[:], mhalf[:], ALU.pow).then_inc(dinv_root, 1)
                    pool.wait_ge(var_ready, t + 1)
                    pool.tensor_tensor(rstd[:], vpe[:], mhalf[:], ALU.pow).then_inc(rstd_ready, 1)
                with pool.Fori(T, 2 * T) as t:
                    pool.wait_ge(var_ready, t + 1)
                    pool.tensor_tensor(rstd[:], vpe[:], mhalf[:], ALU.pow).then_inc(rstd_ready, 1)

        @block.vector
        def _(dve):
            with where_needed(dve):
                dve.memset(mhalf[:], -0.5).then_inc(const_set, 1)
                dve.memset(zeros[:], 0.0).then_inc(const_set, 1)
                dve.wait_ge(wT_ready, 1)
                dve.tensor_copy(w0T[:], tb[:, 0, 0:P]).then_inc(wT_sb, 1)
                dve.tensor_copy(w1T[:], tb[:, 0, P:2 * P]).then_inc(wT_sb, 1)
                dve.wait_ge(wa_ready, 1)
                dve.wait_ge(const_set, 2)
                dve.tensor_copy(w0[:, F:FE], acc[:, 0, 0:2]).then_inc(wa_sb, 1)
                dve.tensor_scalar(wa2[:], zeros[:], acc[:, 0, 1:2], None, ALU.add).then_inc(wa_sb, 1)
                for g in range(GROUPS):
                    dve.wait_ge(xT_ready, g + 1)
                    dve.tensor_copy(xT[:, g * SUPER:(g + 1) * SUPER], tb[:, 0, :]).then_inc(xT_sb, 1)
                for g in range(GROUPS):
                    dve.wait_ge(s2_ready, g + 1)
                    dve.tensor_copy(s2_row[:, g * SUPER:(g + 1) * SUPER], tb[:, 0, :]).then_inc(s2_sb, 1)
                for t in range(T):
                    dve.wait_ge(feat_ready, t + 1)
                    dve.tensor_copy(feat[:, t, :], acc[:, 0, 0:FE]).then_inc(feat_sb, 1)
                dve.wait_ge(s2_sb, GROUPS)
                dve.wait_ge(feat_sb, T)

                def moments(n, v):
                    dve.wait_ge(res_ready, n + 1)
                    dve.tensor_reduce(total[:], v, AX_X, ALU.add).then_inc(mean_step, 1)
                    dve.wait_ge(mean_step, n * 4 + 1)
                    dve.tensor_scalar(total[:], total[:], 1.0 / F, None, ALU.mult).then_inc(mean_step, 1)
                    dve.wait_ge(mean_step, n * 4 + 2)
                    dve.tensor_scalar(v, v, total[:, 0:1], None, ALU.subtract).then_inc(mean_step, 1)
                    dve.wait_ge(mean_step, n * 4 + 3)
                    dve.scalar_tensor_tensor(he[:], v, 1.0, v, ALU.mult, ALU.mult, accum_out=sq[:]
                                             ).then_inc(mean_step, 1)
                    dve.wait_ge(mean_step, n * 4 + 4)
                    dve.tensor_scalar(vpe[:], sq[:], 1.0 / F, EPS, ALU.mult, ALU.add).then_inc(var_ready, 1)
                    dve.wait_ge(rstd_ready, n + 1)

                with dve.Fori(0, T) as t:
                    dve.wait_ge(rows_in, t * 16 + 16)
                    dve.tensor_scalar(mask[:], rows[:], 0.0, None, ALU.is_gt).then_inc(masked, 1)
                    s1 = feat[:, bass.ds(t, 1), F:F + 1].rearrange("p o f -> p (o f)")
                    dve.tensor_scalar(e[:], s2_row[:], s1, None, ALU.add).then_inc(masked, 1)
                    dve.wait_ge(masked, t * 6 + 2)
                    dve.scalar_tensor_tensor(e[:], e[:], SLOPE, e[:], ALU.mult, ALU.max).then_inc(masked, 1)
                    dve.wait_ge(masked, t * 6 + 3)
                    dve.tensor_tensor(e[:], e[:], mask[:], ALU.mult).then_inc(masked, 1)
                    dve.wait_ge(masked, t * 6 + 4)
                    dve.tensor_scalar(mask[:], mask[:], 1.0, NEG, ALU.subtract, ALU.mult).then_inc(masked, 1)
                    dve.wait_ge(masked, t * 6 + 5)
                    dve.tensor_tensor(e[:], e[:], mask[:], ALU.add).then_inc(masked, 1)
                    dve.wait_ge(masked, t * 6 + 6)
                    dve.tensor_reduce(negmax[:], e[:], AX_X, ALU.max, negate=True).then_inc(scores, 1)
                    dve.tensor_reduce(deg[:], rows[:], AX_X, ALU.add).then_inc(rows_used, 1)
                    dve.wait_ge(dinv_root, t + 1)
                    dve.tensor_copy(dinv[:, bass.ds(t, 1)], deg_root[:]).then_inc(dinv_sb, 1)
                    dve.wait_ge(probs, t + 1)
                    dve.reciprocal(rden[:], den[:]).then_inc(rden_sb, 1)
                    dve.wait_ge(rden_sb, t + 1)
                    dve.wait_ge(multiplied, t * GROUPS + GROUPS)
                    dve.tensor_scalar(h[:], acc[:, 0, 0:F], rden[:, 0:1], None, ALU.mult).then_inc(h_ready, 1)
                    dve.wait_ge(h_ready, t + 1)
                    dve.tensor_scalar(he[:], h[:], 0.0, None, ALU.min).then_inc(neg_made, 1)
                    dve.wait_ge(elu_exp, t + 1)
                    dve.scalar_tensor_tensor(h[:], h[:], 0.0, he[:], ALU.max, ALU.add).then_inc(elu_sum, 1)
                    dve.wait_ge(elu_sum, t + 1)
                    dve.scalar_tensor_tensor(h[:], h[:], -1.0, one(x_sb, t), ALU.add, ALU.add).then_inc(res_ready, 1)
                    moments(t, h[:])
                    dve.tensor_scalar(one(x1, t), h[:], rstd[:, 0:1], None, ALU.mult).then_inc(x1_ready, 1)
                    dve.wait_ge(x1_ready, t + 1)
                    dve.wait_ge(dinv_sb, t + 1)
                    dve.tensor_scalar(one(y, t), one(x1, t), dinv[:, bass.ds(t, 1)], None, ALU.mult
                                      ).then_inc(y_ready, 1)
                dve.wait_ge(y_ready, T)

                def layer1(t):
                    dve.wait_ge(z_ready, t + 1)
                    dve.scalar_tensor_tensor(o[:], acc[:, 1, 0:F], dinv[:, bass.ds(t, 1)], one(x1, t),
                                             ALU.mult, ALU.add).then_inc(res_ready, 1)
                    moments(t + T, o[:])
                    dve.tensor_scalar(o[:], o[:], rstd[:, 0:1], None, ALU.mult).then_inc(o_ready, 1)

                layer1(0)
                with dve.Fori(1, T) as t:
                    dve.wait_ge(out_st, t * 16)
                    layer1(t)


def build(nc, x, adj, w_gat, a_gat, w_gcn, ident, out):
    with ExitStack() as ctx:
        flag = ctx.enter_context(nc.sbuf_tensor("flag", [1, 1], I32))
        build_common(nc, x, adj, w_gat, a_gat, w_gcn, ident, out, flag)
        build_general(nc, x, adj, w_gat, a_gat, w_gcn, ident, out, flag)


_INS = ["x", "adj", "L0_gnn_W", "L0_gnn_a", "L1_gnn_W"]


def kernel(**inputs):
    import concourse.bacc as _bacc
    from concourse.bass_utils import run_bass_kernel_spmd as _run

    nc = _bacc.Bacc("TRN2", target_bir_lowering=False, num_devices=1)
    arrays, args = {}, []
    for name in _INS:
        a = np.ascontiguousarray(inputs[name])
        arrays[f"in_{name}"] = a
        args.append(nc.dram_tensor(f"in_{name}", a.shape, mybir.dt.from_np(a.dtype), kind="ExternalInput").ap())
    arrays["in_ident"] = np.eye(P, dtype=np.float32)
    ident = nc.dram_tensor("in_ident", (P, P), F32, kind="ExternalInput").ap()
    out = nc.dram_tensor("out_0", inputs["x"].shape, F32, kind="ExternalOutput").ap()
    build(nc, *args, ident, out)
    r = _run(nc, [arrays], core_ids=[0])
    return r.results[0]["out_0"]
```
